# Optimizing a Trainium2 kernel written in Bass

```python
import numpy as np
import jax
import jax.numpy as jnp

def _softmax(x, axis=-1):
    return jax.nn.softmax(x, axis=axis)

def _gelu(x):
    return jax.nn.gelu(x, approximate=True)

def _silu(x):
    return jax.nn.silu(x)

def _sigmoid(x):
    return jax.nn.sigmoid(x)

def _layernorm(x, axis=-1, eps=1e-05):
    m = jnp.mean(x, axis=axis, keepdims=True)
    v = jnp.var(x, axis=axis, keepdims=True)
    return (x - m) / jnp.sqrt(v + eps)

def _scatter_add(tgt, idx, src, axis=0):
    return tgt.at[idx].add(src)

def _segment_sum(src, seg, n):
    return jax.ops.segment_sum(src, seg, n)
kernel_name = 'mk_gnn_resnorm_d1_gnn_r32_ac944c'

def setup_inputs(seed: int=0):
    np.random.seed(seed)
    _w = jnp.asarray

    def _rec_inputs():
        import jax
        import jax.numpy as jnp
        _gk = jax.random.key(seed)
        x = -8.776e-05 + 1 * jax.random.normal(jax.random.fold_in(_gk, 1), (10000, 512), jnp.float32)
        src = jax.random.randint(jax.random.fold_in(_gk, 2), (5000,), 0, 10000, jnp.int32)
        dst = jnp.minimum((10000 * jax.random.uniform(jax.random.fold_in(_gk, 3), (5000,)) ** 2.0).astype(jnp.int32), 9999)
        _o = jnp.argsort(dst, stable=True)
        src = src[_o]
        dst = dst[_o]
        edge_attr_128 = 1.36993e-05 + 0.999972 * jax.random.normal(jax.random.fold_in(_gk, 11), (5000, 128), jnp.float32)
        return (x, src, dst, edge_attr_128)
    x, src, dst, edge_attr_128 = _rec_inputs()

    def _L0_gnn_setup():
        import jax, jax.numpy as jnp
        import numpy as np
        N_NODES = 10000
        key = jax.random.key(seed)
        ks = jax.random.split(key, 12)
        H, R, E = (512, 128, 5000)
        s = lambda fan_in: 1.0 / np.sqrt(fan_in)
        return {'x': jax.random.normal(ks[0], (N_NODES, H), dtype=jnp.float32), 'edge_rbf': jax.random.normal(ks[1], (E, R), dtype=jnp.float32), 'We1': jax.random.uniform(ks[2], (R, H), jnp.float32, -s(R), s(R)), 'be1': jax.random.uniform(ks[3], (H,), jnp.float32, -s(R), s(R)), 'We2': jax.random.uniform(ks[4], (H, H), jnp.float32, -s(H), s(H)), 'be2': jax.random.uniform(ks[5], (H,), jnp.float32, -s(H), s(H)), 'Wn1': jax.random.uniform(ks[6], (H, H), jnp.float32, -s(H), s(H)), 'bn1': jax.random.uniform(ks[7], (H,), jnp.float32, -s(H), s(H)), 'Wn2': jax.random.uniform(ks[8], (H, H), jnp.float32, -s(H), s(H)), 'bn2': jax.random.uniform(ks[9], (H,), jnp.float32, -s(H), s(H)), 'edge_index': jax.random.randint(ks[10], (2, E), 0, N_NODES, dtype=jnp.int64)}
    _L0_gnn_all = _L0_gnn_setup()
    _L0_gnn_in = {k: v for k, v in _L0_gnn_all.items() if k in ('We1', 'be1', 'We2', 'be2', 'Wn1', 'bn1', 'Wn2', 'bn2')}
    del _L0_gnn_all
    return {'x': x, 'src': src, 'dst': dst, 'edge_attr_128': edge_attr_128, 'L0_gnn_We1': _L0_gnn_in['We1'], 'L0_gnn_be1': _L0_gnn_in['be1'], 'L0_gnn_We2': _L0_gnn_in['We2'], 'L0_gnn_be2': _L0_gnn_in['be2'], 'L0_gnn_Wn1': _L0_gnn_in['Wn1'], 'L0_gnn_bn1': _L0_gnn_in['bn1'], 'L0_gnn_Wn2': _L0_gnn_in['Wn2'], 'L0_gnn_bn2': _L0_gnn_in['bn2']}

def reference(x, src, dst, edge_attr_128, L0_gnn_We1, L0_gnn_be1, L0_gnn_We2, L0_gnn_be2, L0_gnn_Wn1, L0_gnn_bn1, L0_gnn_Wn2, L0_gnn_bn2):
    import jax
    import jax.numpy as jnp

    def _L0_gnn_ref(x, edge_rbf, We1, be1, We2, be2, Wn1, bn1, Wn2, bn2, edge_index):
        import jax, jax.numpy as jnp
        import numpy as np
        N_NODES = 10000
        row, col = (edge_index[0], edge_index[1])
        edge_feature = jax.nn.silu(edge_rbf @ We1 + be1) @ We2 + be2
        msg = edge_feature * x[col]
        agg = jax.ops.segment_sum(msg, row, num_segments=N_NODES)
        return x + (jax.nn.silu(agg @ Wn1 + bn1) @ Wn2 + bn2)
    edge_index = jnp.stack([src, dst])
    x = _layernorm(x + _L0_gnn_ref(x, edge_attr_128, L0_gnn_We1, L0_gnn_be1, L0_gnn_We2, L0_gnn_be2, L0_gnn_Wn1, L0_gnn_bn1, L0_gnn_Wn2, L0_gnn_bn2, edge_index), axis=-1)
    return x

_drawn_inputs = setup_inputs


def setup_inputs(seed=0):
    import zlib

    import numpy as np

    out = dict(_drawn_inputs(seed))
    spreads = {}
    factors = {'edge_attr_128': 5.415,
     'L0_gnn_We1': 5.422,
     'L0_gnn_be1': 32.461,
     'L0_gnn_We2': 5.245,
     'L0_gnn_be2': 64.0,
     'L0_gnn_Wn1': 5.185,
     'L0_gnn_bn1': 8.0,
     'L0_gnn_Wn2': 4.873,
     'L0_gnn_bn2': 4.456}
    for name, (base, spread) in spreads.items():
        noise = np.random.default_rng([zlib.crc32(name.encode()), seed]).standard_normal(out[name].shape)
        drawn = base * np.exp(spread * noise) if base else spread * noise
        out[name] = jnp.asarray(drawn.astype(out[name].dtype))
    for name, factor in factors.items():
        out[name] = (out[name] * factor).astype(out[name].dtype)
    return out
```

```python
from contextlib import ExitStack

import concourse.bass as bass
from concourse import mybir

F32 = mybir.dt.float32
F32R = mybir.dt.float32r
BF16 = mybir.dt.bfloat16
I32 = mybir.dt.int32
ALU = mybir.AluOpType
ACT = mybir.ActivationFunctionType

P = 128
EPS = 1e-5
FAR = 16384


def gnn_kernel(nc, x, src, dst, edge_attr, we1, be1, we2, be2, wn1, bn1, wn2, bn2, out):
    N, H = x.shape
    E, R = edge_attr.shape
    assert R == P and H % P == 0 and H <= 512 and N < FAR
    C = H // P
    J = 4
    M = J * P
    MACROS = -(-E // M)
    TILES = MACROS * J
    PAIRS = MACROS // 2
    assert MACROS % 2 == 0 and PAIRS >= 3
    NT = -(-N // P)
    assert 2 * J * (MACROS - 1) < NT <= 2 * J * MACROS and NT <= TILES * 2
    RT = 40
    RP = E // RT
    assert RP * RT == E and RP <= P and RT % 8 == 0
    HI = 80
    assert NT <= HI
    CENTRE = E // 2
    assert CENTRE < 4096
    VALS = 6

    with ExitStack() as ctx:
        def sb(name, shape, dt=F32, stack=ctx):
            return stack.enter_context(nc.sbuf_tensor(name, shape, dt))

        def sem(name):
            return ctx.enter_context(nc.semaphore(name))

        bank = [ctx.enter_context(nc.psum_tensor(f"bank{n}", [P, 512], F32)) for n in range(8)]

        we1_hi, we1_lo = sb("we1_hi", [P, H], F32R), sb("we1_lo", [P, H], F32R)
        we2_hi, we2_lo = sb("we2_hi", [P, C, H], F32R), sb("we2_lo", [P, C, H], F32R)
        wn1_hi, wn1_lo = sb("wn1_hi", [P, C, H], F32R), sb("wn1_lo", [P, C, H], F32R)
        wn2_hi, wn2_lo = sb("wn2_hi", [P, C, H], F32R), sb("wn2_lo", [P, C, H], F32R)
        be1_col, be2_col, bn1_col = sb("be1_col", [P, C]), sb("be2_col", [P, C]), sb("bn1_col", [P, C])
        bn2_half = sb("bn2_half", [P, H])
        row_half = sb("row_half", [P, H])
        ident, ident_bf = sb("ident", [P, P]), sb("ident_bf", [P, P], BF16)
        minus_half = sb("minus_half", [P, J])
        gather_index = sb("gather_index", [P, 3, TILES], I32)
        store_index = sb("store_index", [P, TILES], I32)
        base_index = sb("base_index", [P, 2 * TILES], I32)
        same_as_before = sb("same_as_before", [P, TILES], BF16)
        carry = sb("carry", [P, C])

        with ExitStack() as early:
            def eb(name, shape, dt=F32):
                return sb(name, shape, dt, early)

            src_row = eb("src_row", [RP, E], I32)
            edge_int = eb("edge_int", [RP, 3, RT], I32)
            part_int = eb("part_int", [RP, VALS, RT], I32)
            vals = eb("vals", [RP, RT, VALS], BF16)
            src_f, hi_f, lo_f = eb("src_f", [RP, RT]), eb("hi_f", [RP, RT]), eb("lo_f", [RP, RT])
            iota_int, iota_f = eb("iota_int", [P, P], I32), eb("iota_f", [P, P])
            node_int, node_f = eb("node_int", [P, 2 * TILES], I32), eb("node_f", [P, 2 * TILES])
            earlier = eb("earlier", [P, P])
            later = eb("later", [P, P])
            take_next, wrap_next = eb("take_next", [P, P]), eb("wrap_next", [P, P])
            take_prev, wrap_prev = eb("take_prev", [P, P]), eb("wrap_prev", [P, P])
            pad_far = eb("pad_far", [P, 1])
            is_lo = eb("is_lo", [RP, RT, P], BF16)
            is_hi = eb("is_hi", [RP, RT, HI], BF16)
            is_hi_T = eb("is_hi_T", [HI, RT, P], F32R)
            start_of = eb("start_of", [HI, RT + 1, P], F32R)
            total, total_T = eb("total", [HI, P]), eb("total_T", [P, HI])
            row_sum, row_sum_b = eb("row_sum", [HI, 1]), eb("row_sum_b", [HI, P])
            touched = eb("touched", [P, HI])
            within, found = eb("within", [RP, RT]), eb("found", [RP, RT])
            scrap = eb("scrap", [RP, 2, 4, P])
            pos_f, pos_int = eb("pos_f", [RP, RT]), eb("pos_int", [RP, 3, RT], I32)
            pos_part = eb("pos_part", [RP, 2, RT])
            is_slot = eb("is_slot", [RP, 8, P], BF16)
            is_tile = eb("is_tile", [RP, 8, TILES], BF16)
            spread = eb("spread", [RP, 8, VALS, TILES], BF16)
            sorted_parts = eb("sorted_parts", [P, VALS, TILES])
            src_sorted = eb("src_sorted", [P, TILES + 2])
            same_as_next = eb("same_as_next", [P, TILES])
            raw = [eb(f"raw{n}", [P, (1 if n == 0 else C) * H]) for n in range(4)]
            bn2_row = eb("bn2_row", [P, H])
            mid_hi, mid_lo = eb("mid_hi", [P, C, P], F32R), eb("mid_lo", [P, C, P], F32R)
            mid = eb("mid", [P, C, P])

        attr = sb("attr", [P, 2, J, R])
        xd = sb("xd", [P, 2, J, H])
        xs = sb("xs", [P, J, H])
        z = sb("z", [P, J, H])
        attr_T_hi, attr_T_lo = sb("attr_T_hi", [P, M], F32R), sb("attr_T_lo", [P, M], F32R)
        h_hi, h_lo = sb("h_hi", [P, C, M], F32R), sb("h_lo", [P, C, M], F32R)
        u_hi, u_lo = sb("u_hi", [P, C, M], F32R), sb("u_lo", [P, C, M], F32R)
        agg_hi, agg_lo = sb("agg_hi", [P, C, M], F32R), sb("agg_lo", [P, C, M], F32R)
        xd_T = sb("xd_T", [P, C, M])
        msg_T = sb("msg_T", [P, 2, M])
        agg_T = sb("agg_T", [P, 2, M])
        silu = sb("silu", [P, 2, M])
        base = sb("base", [P, 2, 2, J, H])
        gather_now = sb("gather_now", [P, 2, 2, J], I32)
        own_now = sb("own_now", [P, 2, J], I32)
        store_now = sb("store_now", [P, 2, J], I32)
        base_now = sb("base_now", [P, 2, 2, J], I32)
        stats = sb("stats", [P, 3, J, 6])
        mean_var = sb("mean_var", [P, 3, J, 2])
        var_eps, rstd = sb("var_eps", [P, 3, J]), sb("rstd", [P, 3, J])
        mean_r, shift = sb("mean_r", [P, 3, J]), sb("shift", [P, 3, J])
        OUT, HALF_A, HALF_B = 0, 1, 2

        s = {name: sem(name) for name in (
            "src_in dst_in src_row_in be1_in be2_in bn1_in bn2_in we1_in we2_in wn1_in wn2_in "
            "pool_const we_hi wn_hi we_lo wn_lo bn2_halved mid_split mid_low row_mm row_ready "
            "parts one_hots totals_mm totals_copied sums_chain start_mm start0 tile_mm chained hi_T_mm hi_T_ready "
            "find_mm found_done within_done rank_chain spread_ready index_mm index_chain src_sorted_ready "
            "shift_mm index_ready base_index_ready spread_used "
            "attr_T_mm attr_T_hi_ready attr_T_lo_ready h_mm h_silu h_lo_ready ef_mm msg_ready scan_done carried "
            "agg_hi_ready agg_lo_ready u_mm u_silu u_lo_ready xd_T_mm xd_T_ready mask_mm y_mm z_ready "
            "dve_stats_out dve_stats_a dve_stats_b base_added_a base_added_b aggr_out aggr_a aggr_b "
            "rows_out rows_a rows_b moments_chain copied_gather copied_own copied_store copied_base "
            "xs_biased xs_in out_stored passed"
        ).split()}
        attr_in = [sem(f"attr_in{b}") for b in range(2)]
        xd_in = [sem(f"xd_in{b}") for b in range(2)]
        base_in = [[sem(f"base_in{b}{h}") for h in range(2)] for b in range(2)]
        base_stored = [[sem(f"base_stored{b}{h}") for h in range(2)] for b in range(2)]

        def need(eng, name, count, alone=False):
            if isinstance(count, int) and count <= 0:
                return
            eng.wait_ge(s[name] if isinstance(name, str) else name, count)
            if alone and not isinstance(count, int):
                eng.sem_inc(s["passed"], 1)

        def steps(eng, step):
            for b in range(2):
                step(b, 0, b)
            with eng.Fori(1, PAIRS - 1) as i:
                for b in range(2):
                    step(2 * i + b, i, b)
            for b in range(2):
                step(MACROS - 2 + b, PAIRS - 1, b)

        def is_last(m):
            return isinstance(m, int) and m == MACROS - 1

        def base_rows(m, half, k):
            if not isinstance(m, int):
                return P
            return max(0, min(P, N - ((2 * m + half) * J + k) * P))

        def hi_T_bank(g):
            return bank[(2, 7)[g % 2]][0:HI, 0:256].bitcast(BF16).rearrange("p (k e) -> p k e", k=4)[:, :, 0:RP]

        def moments_made(which, m):
            return 12 * m + {HALF_A: 4, HALF_B: 8, OUT: 12}[which]

        block = ctx.enter_context(nc.Block())

        @block.sync
        def _(sp):
            sp.dma_start(edge_int[:, 2, :], src.rearrange("(p t) -> p t", t=RT)).then_inc(s["src_in"], 16)
            sp.dma_start(edge_int[:, 1, :], dst.rearrange("(p t) -> p t", t=RT)).then_inc(s["dst_in"], 16)
            sp.dma_start(raw[0][:, :], we1).then_inc(s["we1_in"], 16)
            for w, r, name in ((we2, raw[1], "we2_in"), (wn2, raw[3], "wn2_in"), (wn1, raw[2], "wn1_in")):
                sp.dma_start(r[:, :].rearrange("p (c n) -> p c n", c=C),
                             w.rearrange("(c p) n -> p c n", p=P)).then_inc(s[name], 16)
            sp.wait_ge(s["index_ready"], 1)
            sp.wait_ge(s["row_ready"], 1)
            sp.wait_ge(s["wn_lo"], 2)

            def step(m, i, b):
                for half in range(2):
                    need(sp, base_stored[b][half], 64 * i)
                    first = (2 * m + half) * J * P
                    full = sum(base_rows(m, half, k) == P for k in range(J))
                    sp.dma_start(base[:, b, half, 0:full, :],
                                 x[bass.ds(first, full * P), :].rearrange("(k p) h -> p k h", p=P)
                                 ).then_inc(base_in[b][half], 16)
                    if full < J and base_rows(m, half, full):
                        n = base_rows(m, half, full)
                        sp.dma_start(base[0:n, b, half, full, :], x[N - n:N, :]).then_inc(base_in[b][half], 16)

            steps(sp, step)

        @block.gpsimd
        def _(pool):
            consts = [0]

            def const(ins):
                ins.then_inc(s["pool_const"], 1)
                consts[0] += 1

            for t in (ident, ident_bf, take_next, wrap_next, take_prev, wrap_prev):
                const(nc.gpsimd.memset(t[:, :], 0.0))
            for t in (earlier, later):
                const(nc.gpsimd.memset(t[:, :], 1.0))
            const(nc.gpsimd.memset(pad_far[:, :], float(FAR)))
            const(nc.gpsimd.memset(minus_half[:, :], -0.5))
            const(nc.gpsimd.memset(carry[:, :], 0.0))
            const(nc.gpsimd.memset(src_sorted[:, :], -1.0))
            const(nc.gpsimd.iota(iota_int[:, :], [[1, P]], base=0, channel_multiplier=0))
            const(nc.gpsimd.iota(node_int[:, :], [[P, 2 * TILES]], base=0, channel_multiplier=1))
            const(nc.gpsimd.iota(edge_int[:, 0, :], [[1, RT]], base=0, channel_multiplier=RT))
            pool.wait_ge(s["pool_const"], consts[0])
            for t, at in ((ident, 0), (ident_bf, 0), (take_next, -1), (wrap_next, P - 1), (take_prev, 1),
                          (wrap_prev, -(P - 1))):
                const(nc.gpsimd.affine_select(out=t[:, :], in_=t[:, :], compare_op=ALU.not_equal, fill=1.0,
                                              base=at, pattern=[[-1, P]], channel_multiplier=1))
            const(nc.gpsimd.affine_select(out=earlier[:, :], in_=earlier[:, :], compare_op=ALU.is_gt, fill=0.0,
                                          base=0, pattern=[[-1, P]], channel_multiplier=1))
            const(nc.gpsimd.affine_select(out=later[:, :], in_=later[:, :], compare_op=ALU.is_gt, fill=0.0,
                                          base=0, pattern=[[1, P]], channel_multiplier=-1))
            const(nc.gpsimd.affine_select(out=pad_far[:, :], in_=pad_far[:, :], compare_op=ALU.is_ge, fill=0.0,
                                          base=-(E - (TILES - 1) * P), pattern=[[0, 1]], channel_multiplier=1))
            assert consts[0] == POOL_CONSTS

            pool.wait_ge(s["we_hi"], 1)
            nc.gpsimd.tensor_tensor(we1_lo[:, :], raw[0][:, :], we1_hi[:, :].bitcast(F32),
                                    ALU.subtract).then_inc(s["we_lo"], 1)
            pool.wait_ge(s["we_hi"], 2)
            nc.gpsimd.tensor_tensor(we2_lo[:, :, :].rearrange("p c n -> p (c n)"), raw[1][:, :],
                                    we2_hi[:, :, :].rearrange("p c n -> p (c n)").bitcast(F32),
                                    ALU.subtract).then_inc(s["we_lo"], 1)
            pool.wait_ge(s["mid_split"], 1)
            nc.gpsimd.tensor_tensor(mid_lo[:, :, :].rearrange("p c n -> p (c n)"),
                                    mid[:, :, :].rearrange("p c n -> p (c n)"),
                                    mid_hi[:, :, :].rearrange("p c n -> p (c n)").bitcast(F32),
                                    ALU.subtract).then_inc(s["mid_low"], 1)
            for n, (hi, lo, r) in enumerate(((wn2_hi, wn2_lo, raw[3]), (wn1_hi, wn1_lo, raw[2]))):
                pool.wait_ge(s["wn_hi"], n + 1)
                nc.gpsimd.tensor_tensor(lo[:, :, :].rearrange("p c n -> p (c n)"), r[:, :],
                                        hi[:, :, :].rearrange("p c n -> p (c n)").bitcast(F32),
                                        ALU.subtract).then_inc(s["wn_lo"], 1)

            pool.wait_ge(s["index_ready"], 1)
            pool.wait_ge(s["row_ready"], 1)

            def gather_edges(m, i, b):
                need(pool, "attr_T_mm", m - 1, True)
                need(pool, "xd_T_mm", C * (m - 1), True)
                nc.gpsimd.tensor_copy(gather_now[:, b, :, :], gather_index[:, 0:2, bass.ds(m * J, J)]
                                      ).then_inc(s["copied_gather"], 1)
                need(pool, "copied_gather", m + 1, True)
                for j in range(J):
                    pool.indirect_dma_start(
                        out=attr[:, b, j, :], out_offset=None, in_=edge_attr,
                        in_offset=bass.IndirectOffsetOnAxis(ap=gather_now[:, b, 0, j:j + 1], axis=0),
                    ).then_inc(attr_in[b], 16)
                for j in range(J):
                    pool.indirect_dma_start(
                        out=xd[:, b, j, :], out_offset=None, in_=x,
                        in_offset=bass.IndirectOffsetOnAxis(ap=gather_now[:, b, 1, j:j + 1], axis=0),
                    ).then_inc(xd_in[b], 16)

            def moments(which, m, aggr, rows, tiles, eps):
                c = moments_made(which, m) - 4
                need(pool, aggr, J * m + tiles, True)
                need(pool, rows, J * m, True)
                nc.gpsimd.tensor_scalar(out=var_eps[:, which, :], in0=mean_var[:, which, :, 1], scalar1=eps,
                                        scalar2=None, op0=ALU.add).then_inc(s["moments_chain"], 1)
                need(pool, "moments_chain", c + 1, True)
                nc.gpsimd.tensor_tensor(rstd[:, which, :], var_eps[:, which, :], minus_half[:, :],
                                        ALU.pow).then_inc(s["moments_chain"], 1)
                need(pool, "moments_chain", c + 2, True)
                nc.gpsimd.tensor_tensor(mean_r[:, which, :], mean_var[:, which, :, 0], rstd[:, which, :],
                                        ALU.mult).then_inc(s["moments_chain"], 1)
                need(pool, "moments_chain", c + 3, True)
                nc.gpsimd.tensor_scalar(out=shift[:, which, :], in0=mean_r[:, which, :], scalar1=-1.0,
                                        scalar2=None, op0=ALU.mult).then_inc(s["moments_chain"], 1)

            def store_base(m, i, b, half, rows):
                for k in range(J):
                    n = base_rows(m, half, k)
                    if n:
                        need(pool, rows, J * m + k + 1, True)
                        pool.indirect_dma_start(
                            out=out, in_=base[0:n, b, half, k, :], in_offset=None,
                            out_offset=bass.IndirectOffsetOnAxis(ap=base_now[0:n, b, half, k:k + 1], axis=0),
                            bounds_check=N - 1, oob_is_err=False).then_inc(base_stored[b][half], 16)

            def store_sorted(m, i, b):
                nc.gpsimd.tensor_copy(store_now[:, b, :], store_index[:, bass.ds(m * J, J)]
                                      ).then_inc(s["copied_store"], 1)
                need(pool, "copied_store", m + 1, True)
                for j in range(J):
                    need(pool, "rows_out", J * m + j + 1, True)
                    pool.indirect_dma_start(
                        out=out, in_=z[:, j, :], in_offset=None,
                        out_offset=bass.IndirectOffsetOnAxis(ap=store_now[:, b, j:j + 1], axis=0),
                        bounds_check=N - 1, oob_is_err=False).then_inc(s["out_stored"], 16)

            def finish(m):
                moments(HALF_B, m, "aggr_b", "rows_b", sum(base_rows(m, 1, k) > 0 for k in range(J)), EPS / 4)
                moments(OUT, m, "aggr_out", "rows_out", J, EPS)

            def stores(m, i, b):
                for half in range(2):
                    need(pool, base_stored[b][half], 16 * J * i, True)
                need(pool, "out_stored", 16 * J * (m - 1), True)
                nc.gpsimd.tensor_copy(base_now[:, b, :, :], base_index[:, bass.ds(m * 2 * J, 2 * J)]
                                      .rearrange("p (h k) -> p h k", h=2)).then_inc(s["copied_base"], 1)
                need(pool, "copied_base", m + 1, True)
                store_base(m, i, b, 0, "rows_a")
                store_base(m, i, b, 1, "rows_b")
                store_sorted(m, i, b)

            gather_edges(0, 0, 0)
            gather_edges(1, 0, 1)

            def step(m, i, b):
                if not (isinstance(m, int) and m == 0):
                    finish(m - 1)
                need(pool, "z_ready", J * m, True)
                nc.gpsimd.tensor_copy(own_now[:, b, :], gather_index[:, 2, bass.ds(m * J, J)]
                                      ).then_inc(s["copied_own"], 1)
                need(pool, "copied_own", m + 1, True)
                for j in range(J):
                    pool.indirect_dma_start(
                        out=xs[:, j, :], out_offset=None, in_=x,
                        in_offset=bass.IndirectOffsetOnAxis(ap=own_now[:, b, j:j + 1], axis=0),
                    ).then_inc(s["xs_in"], 16)
                if not (isinstance(m, int) and m >= MACROS - 2):
                    gather_edges(m + 2, i + 1, b)
                need(pool, "xs_in", 16 * J * (m + 1), True)
                for j in range(J):
                    nc.gpsimd.tensor_tensor(xs[:, j, :], xs[:, j, :], bn2_half[:, :], ALU.add
                                            ).then_inc(s["xs_biased"], 1)
                if not (isinstance(m, int) and m == 0):
                    stores(m - 1, i if b else i - 1, 1 - b)
                moments(HALF_A, m, "aggr_a", "rows_a", J, EPS / 4)

            steps(pool, step)
            last = MACROS - 1
            finish(last)
            stores(last, PAIRS - 1, 1)
            need(pool, "out_stored", 16 * TILES, True)
            for b in range(2):
                for half in range(2):
                    tiles = sum(base_rows(m, half, k) > 0 for m in range(b, MACROS, 2) for k in range(J))
                    pool.wait_ge(base_stored[b][half], 16 * tiles)

        @block.scalar
        def _(act):
            act.dma_start(src_row[:, :], src.rearrange("(o e) -> o e", o=1).broadcast_to([RP, E])
                          ).then_inc(s["src_row_in"], 16)
            act.dma_start(bn2_row[:, :], bn2.rearrange("(o h) -> o h", o=1).broadcast_to([P, H])
                          ).then_inc(s["bn2_in"], 16)
            for v, t, name in ((be1, be1_col, "be1_in"), (be2, be2_col, "be2_in"), (bn1, bn1_col, "bn1_in")):
                act.dma_start(t[:, :], v.rearrange("(c p) -> p c", p=P), allow_slow_non_contiguous=True
                              ).then_inc(s[name], 16)
            act.wait_ge(s["we1_in"], 16)
            nc.scalar.activation(we1_hi[:, :], raw[0][:, :], ACT.Copy).then_inc(s["we_hi"], 1)
            act.wait_ge(s["we2_in"], 16)
            nc.scalar.activation(we2_hi[:, :, :].rearrange("p c n -> p (c n)"), raw[1][:, :], ACT.Copy
                                 ).then_inc(s["we_hi"], 1)
            act.wait_ge(s["bn1_in"], 16)
            bn1_wide = bn1_col[:, :].unsqueeze(2).broadcast_to([P, C, P])
            nc.scalar.activation(mid_hi[:, :, :], bn1_wide, ACT.Silu)
            nc.scalar.activation(mid[:, :, :], bn1_wide, ACT.Silu).then_inc(s["mid_split"], 1)
            act.wait_ge(s["bn2_in"], 16)
            nc.scalar.activation(bn2_half[:, :], bn2_row[:, :], ACT.Copy, scale=0.5).then_inc(s["bn2_halved"], 1)
            for name, hi, r in (("wn2_in", wn2_hi, raw[3]), ("wn1_in", wn1_hi, raw[2])):
                act.wait_ge(s[name], 16)
                nc.scalar.activation(hi[:, :, :].rearrange("p c n -> p (c n)"), r[:, :], ACT.Copy
                                     ).then_inc(s["wn_hi"], 1)
            for g in range(RT // 4):
                act.wait_ge(s["hi_T_mm"], g + 1)
                nc.scalar.activation(is_hi_T[:, 4 * g:4 * g + 4, 0:RP],
                                     hi_T_bank(g), ACT.Copy).then_inc(s["hi_T_ready"], 1)

            def split_attr(m):
                act.wait_ge(s["attr_T_mm"], m + 1)
                need(act, "h_mm", C * m)
                nc.scalar.activation(attr_T_hi[:, :], bank[4][:, :], ACT.Copy).then_inc(s["attr_T_hi_ready"], 1)

            def hidden(m):
                for c in range(C):
                    act.wait_ge(s["h_mm"], C * m + c + 1)
                    if c == 0:
                        need(act, "ef_mm", C * m)
                    if c >= 2:
                        need(act, "h_lo_ready", C * m + c - 1)
                    else:
                        need(act, "u_lo_ready", C * (m - 2) + c + 3)
                    nc.scalar.activation(h_hi[:, c, :], bank[c][:, :], ACT.Silu, bias=be1_col[:, c:c + 1])
                    nc.scalar.activation(silu[:, c % 2, :], bank[c][:, :], ACT.Silu, bias=be1_col[:, c:c + 1]
                                         ).then_inc(s["h_silu"], 1)

            def transposed_rows(m):
                for c in range(C):
                    act.wait_ge(s["xd_T_mm"], C * m + c + 1)
                    need(act, "msg_ready", C * (m - 1) + c + 1)
                    nc.scalar.activation(xd_T[:, c, :], bank[5 + c % 2][:, :], ACT.Copy
                                         ).then_inc(s["xd_T_ready"], 1)

            def norm_base(m, b, half, k, which, rows):
                n = base_rows(m, half, k)
                if n:
                    if k == 0:
                        act.wait_ge(s["moments_chain"], moments_made(which, m))
                    t = base[0:n, b, half, k, :]
                    nc.scalar.activation(t, t, ACT.Identity, bias=shift[0:n, which, k:k + 1],
                                         scale=rstd[0:n, which, k:k + 1]).then_inc(s[rows], 1)

            def norm_sorted(m, j):
                if j == 0:
                    act.wait_ge(s["moments_chain"], moments_made(OUT, m))
                nc.scalar.activation(z[:, j, :], z[:, j, :], ACT.Identity, bias=shift[:, OUT, j:j + 1],
                                     scale=rstd[:, OUT, j:j + 1]).then_inc(s["rows_out"], 1)

            act.wait_ge(s["be1_in"], 16)
            split_attr(0)
            hidden(0)
            transposed_rows(0)

            def step(m, i, b):
                first = isinstance(m, int) and m == 0
                for c in range(C):
                    act.wait_ge(s["scan_done"], C * m + c + 1)
                    if c == 0:
                        need(act, "u_mm", C * m)
                    nc.scalar.activation(agg_hi[:, c, :], agg_T[:, c % 2, :], ACT.Copy
                                         ).then_inc(s["agg_hi_ready"], 1)
                    if not first:
                        norm_base(m - 1, 1 - b, 1, c, HALF_B, "rows_b")
                        norm_sorted(m - 1, c)
                if not is_last(m):
                    split_attr(m + 1)
                    hidden(m + 1)
                for c in range(C):
                    act.wait_ge(s["u_mm"], C * m + c + 1)
                    if c == 0:
                        need(act, "y_mm", C * m)
                    if c >= 2:
                        need(act, "u_lo_ready", C * m + c - 1)
                    elif is_last(m):
                        need(act, "u_lo_ready", C * (m - 1) + c + 3)
                    else:
                        need(act, "h_lo_ready", C * (m + 1) + c + 3)
                    nc.scalar.activation(u_hi[:, c, :], bank[c][:, :], ACT.Silu, bias=bn1_col[:, c:c + 1])
                    nc.scalar.activation(silu[:, c % 2, :], bank[c][:, :], ACT.Silu, bias=bn1_col[:, c:c + 1]
                                         ).then_inc(s["u_silu"], 1)
                if not is_last(m):
                    transposed_rows(m + 1)
                for k in range(J):
                    norm_base(m, b, 0, k, HALF_A, "rows_a")

            steps(act, step)
            for j in range(J):
                norm_base(MACROS - 1, 1, 1, j, HALF_B, "rows_b")
                norm_sorted(MACROS - 1, j)

        def product(pe, target, lhs_hi, lhs_lo, rhs_hi, rhs_lo, start, stop):
            pe.matmul(target, lhs_lo, rhs_hi, start=start, stop=False)
            pe.matmul(target, lhs_hi, rhs_lo, start=False, stop=False)
            return pe.matmul(target, lhs_hi, rhs_hi, start=False, stop=stop)

        @block.tensor
        def _(pe):
            pe.wait_ge(s["pool_const"], POOL_CONSTS)
            pe.wait_ge(s["one_hots"], 2)
            for t in range(RT):
                pe.matmul(bank[4][0:HI, 0:P], is_hi[:, t, :], is_lo[:, t, :], start=(t == 0), stop=(t == RT - 1))
                mm = pe.matmul(bank[5][0:P, 0:HI], is_lo[:, t, :], is_hi[:, t, :], start=(t == 0),
                               stop=(t == RT - 1))
            mm.then_inc(s["totals_mm"], 1)

            def transpose_hi(g):
                need(pe, "hi_T_ready", g - 1)
                for k in range(4):
                    mm = pe.transpose(hi_T_bank(g)[:, k, :], is_hi[:, 4 * g + k, :], ident_bf[0:RP, 0:RP])
                mm.then_inc(s["hi_T_mm"], 1)

            def tile_counts(g):
                need(pe, "chained", 4 * (g - 1))
                for k in range(4):
                    mm = pe.matmul(bank[g % 2][0:HI, P * k:P * k + P], is_hi[:, 4 * g + k, :],
                                   is_lo[:, 4 * g + k, :], start=True, stop=True)
                mm.then_inc(s["tile_mm"], 1)

            transpose_hi(0)
            transpose_hi(1)
            tile_counts(0)
            tile_counts(1)
            pe.wait_ge(s["totals_copied"], 4)
            pe.matmul(bank[6][0:HI, 0:P], total_T[:, :], later[:, :], start=True, stop=False)
            pe.matmul(bank[6][0:HI, 0:P], later[0:HI, 0:HI], row_sum_b[:, :], start=False, stop=True
                      ).then_inc(s["start_mm"], 1)
            for g in range(RT // 4):
                if g >= 2:
                    transpose_hi(g)
                    tile_counts(g)
                pe.wait_ge(s["hi_T_ready"], g + 1)
                need(pe, "found_done", 4 * (g - 1))
                for k in range(4):
                    t = 4 * g + k
                    need(pe, "start0", 1)
                    need(pe, "chained", t)
                    mm = pe.matmul(bank[3 + g % 2][0:RP, P * k:P * k + P], is_hi_T[:, t, 0:RP], start_of[:, t, :],
                                   start=True, stop=True)
                mm.then_inc(s["find_mm"], 1)
            pe.wait_ge(s["mid_low"], 1)
            pe.wait_ge(s["wn_lo"], 1)
            for c in range(C):
                mm = product(pe, bank[5][:, :], mid_hi[:, c, :], mid_lo[:, c, :], wn2_hi[:, c, :],
                             wn2_lo[:, c, :], c == 0, c == C - 1)
            mm.then_inc(s["row_mm"], 1)
            for g in range(RT // 8):
                pe.wait_ge(s["spread_ready"], g + 1)
                for k in range(8):
                    mm = pe.matmul(bank[6][:, 0:VALS * TILES], is_slot[:, k, :],
                                   spread[:, k, :, :].rearrange("p v a -> p (v a)"),
                                   start=(g == 0 and k == 0), stop=(g == RT // 8 - 1 and k == 7))
                mm.then_inc(s["index_mm"], 1)
            pe.wait_ge(s["src_sorted_ready"], 1)
            pe.matmul(bank[7][:, 0:TILES], take_next[:, :], src_sorted[:, 1:TILES + 1], start=True, stop=False)
            pe.matmul(bank[7][:, 0:TILES], wrap_next[:, :], src_sorted[:, 2:TILES + 2], start=False, stop=True
                      ).then_inc(s["shift_mm"], 1)
            pe.matmul(bank[2][:, 0:TILES], take_prev[:, :], src_sorted[:, 1:TILES + 1], start=True, stop=False)
            pe.matmul(bank[2][:, 0:TILES], wrap_prev[:, :], src_sorted[:, 0:TILES], start=False, stop=True
                      ).then_inc(s["shift_mm"], 1)
            pe.wait_ge(s["index_ready"], 1)
            pe.wait_ge(s["row_ready"], 1)
            pe.wait_ge(s["we_lo"], 2)
            pe.wait_ge(s["wn_lo"], 2)

            def attr_transposes(m, i, b):
                pe.wait_ge(attr_in[b], 16 * J * (i + 1))
                need(pe, "attr_T_lo_ready", m)
                for j in range(J):
                    mm = pe.transpose(bank[4][:, P * j:P * j + P], attr[:, b, j, :], ident[:, :])
                mm.then_inc(s["attr_T_mm"], 1)

            def row_transposes(m, i, b):
                pe.wait_ge(xd_in[b], 16 * J * (i + 1))
                for c in range(C):
                    if c >= 2 or not (isinstance(m, int) and m == 0):
                        pe.wait_ge(s["xd_T_ready"], C * m + c - 1)
                    for j in range(J):
                        mm = pe.transpose(bank[5 + c % 2][:, P * j:P * j + P], xd[:, b, j, P * c:P * c + P],
                                          ident[:, :])
                    mm.then_inc(s["xd_T_mm"], 1)

            def mask(m):
                need(pe, "scan_done", C * m)
                for j in range(J):
                    mm = pe.matmul(bank[7][:, P * j:P * j + P],
                                   same_as_before[:, bass.ds(m * J + j, 1)].broadcast_to([P, P]),
                                   ident_bf[:, :], start=True, stop=True)
                mm.then_inc(s["mask_mm"], 1)

            def layer1(m):
                pe.wait_ge(s["attr_T_hi_ready"], m + 1)
                pe.wait_ge(s["attr_T_lo_ready"], m + 1)
                for c in range(C):
                    need(pe, "msg_ready", C * (m - 1) + c + 1)
                    w = slice(P * c, P * c + P)
                    product(pe, bank[c][:, :], we1_hi[:, w], we1_lo[:, w], attr_T_hi[:, :], attr_T_lo[:, :],
                            True, True).then_inc(s["h_mm"], 1)

            attr_transposes(0, 0, 0)
            layer1(0)
            row_transposes(0, 0, 0)
            mask(0)

            def step(m, i, b):
                for c in range(C):
                    if c == C - 1 and not is_last(m):
                        attr_transposes(m + 1, i if b == 0 else i + 1, 1 - b)
                    need(pe, "z_ready", C * (m - 1) + c + 1)
                    for k in range(C):
                        if c == 0:
                            pe.wait_ge(s["h_silu"], C * m + k + 1)
                            pe.wait_ge(s["h_lo_ready"], C * m + k + 1)
                        w = slice(P * c, P * c + P)
                        mm = product(pe, bank[c][:, :], we2_hi[:, k, w], we2_lo[:, k, w], h_hi[:, k, :],
                                     h_lo[:, k, :], k == 0, k == C - 1)
                    mm.then_inc(s["ef_mm"], 1)
                if not is_last(m):
                    layer1(m + 1)
                for c in range(C):
                    if is_last(m):
                        pe.wait_ge(s["msg_ready"], C * m + c + 1)
                    else:
                        pe.wait_ge(s["h_silu"], C * (m + 1) + c + 1)
                    for k in range(C):
                        if c == 0:
                            pe.wait_ge(s["agg_hi_ready"], C * m + k + 1)
                            pe.wait_ge(s["agg_lo_ready"], C * m + k + 1)
                        w = slice(P * c, P * c + P)
                        mm = product(pe, bank[c][:, :], wn1_hi[:, k, w], wn1_lo[:, k, w], agg_hi[:, k, :],
                                     agg_lo[:, k, :], k == 0, k == C - 1)
                    mm.then_inc(s["u_mm"], 1)
                if not is_last(m):
                    row_transposes(m + 1, i if b == 0 else i + 1, 1 - b)
                    mask(m + 1)
                for j in range(J):
                    pe.wait_ge(s["u_silu"], C * m + j + 1)
                    for k in range(C):
                        if j == 0:
                            pe.wait_ge(s["u_silu"], C * m + k + 1)
                            pe.wait_ge(s["u_lo_ready"], C * m + k + 1)
                        w = slice(P * j, P * j + P)
                        mm = product(pe, bank[j][:, :], u_hi[:, k, w], u_lo[:, k, w], wn2_hi[:, k, :],
                                     wn2_lo[:, k, :], k == 0, k == C - 1)
                    mm.then_inc(s["y_mm"], 1)

            steps(pe, step)

        @block.vector
        def _(dve):
            dve.wait_ge(s["pool_const"], POOL_CONSTS)
            dve.wait_ge(s["src_in"], 16)
            dve.wait_ge(s["dst_in"], 16)
            parts4 = part_int[:, :, :].rearrange("p (v h) t -> p v h t", h=2)
            nc.vector.tensor_scalar(parts4[:, :, 0, :], edge_int[:, :, :], 7, None, ALU.logical_shift_right
                                    ).then_inc(s["parts"], 1)
            nc.vector.tensor_scalar(parts4[:, :, 1, :], edge_int[:, :, :], P - 1, None, ALU.bitwise_and
                                    ).then_inc(s["parts"], 1)
            nc.vector.tensor_copy(iota_f[:, :], iota_int[:, :]).then_inc(s["parts"], 1)
            nc.vector.tensor_copy(src_f[:, :], edge_int[:, 2, :]).then_inc(s["parts"], 1)
            dve.wait_ge(s["parts"], 4)
            nc.vector.tensor_copy(hi_f[:, :], part_int[:, 4, :]).then_inc(s["parts"], 1)
            nc.vector.tensor_copy(lo_f[:, :], part_int[:, 5, :]).then_inc(s["parts"], 1)
            dve.wait_ge(s["parts"], 6)
            nc.vector.tensor_tensor(is_hi[:, :, :], iota_f[0:RP, 0:HI].unsqueeze(1).broadcast_to([RP, RT, HI]),
                                    hi_f[:, :].unsqueeze(2).broadcast_to([RP, RT, HI]), ALU.is_equal
                                    ).then_inc(s["one_hots"], 1)
            nc.vector.tensor_tensor(is_lo[:, :, :], iota_f[0:RP, :].unsqueeze(1).broadcast_to([RP, RT, P]),
                                    lo_f[:, :].unsqueeze(2).broadcast_to([RP, RT, P]), ALU.is_equal
                                    ).then_inc(s["one_hots"], 1)
            nc.vector.tensor_copy(vals[:, :, :], part_int[:, :, :].rearrange("p v t -> p t v")
                                  ).then_inc(s["parts"], 1)
            nc.vector.tensor_copy(node_f[:, :], node_int[:, :]).then_inc(s["parts"], 1)
            dve.wait_ge(s["totals_mm"], 1)
            nc.vector.tensor_copy(total[:, :], bank[4][0:HI, 0:P]).then_inc(s["totals_copied"], 1)
            nc.vector.tensor_copy(total_T[:, :], bank[5][0:P, 0:HI]).then_inc(s["totals_copied"], 1)
            dve.wait_ge(s["totals_copied"], 2)
            nc.vector.tensor_reduce(row_sum[:, :], total[:, :], mybir.AxisListType.X, ALU.add
                                    ).then_inc(s["totals_copied"], 1)
            dve.wait_ge(s["totals_copied"], 3)
            nc.vector.tensor_copy(row_sum_b[:, :], row_sum[:, :].broadcast_to([HI, P])
                                  ).then_inc(s["totals_copied"], 1)
            nc.vector.tensor_scalar(touched[:, :], total_T[:, :], 1.0, float(FAR), ALU.min, ALU.mult
                                    ).then_inc(s["base_index_ready"], 1)
            dve.wait_ge(s["base_index_ready"], 1)
            dve.wait_ge(s["parts"], 8)
            nc.vector.tensor_tensor(base_index[:, 0:HI], node_f[:, 0:HI], touched[:, :], ALU.add
                                    ).then_inc(s["base_index_ready"], 1)
            dve.wait_ge(s["start_mm"], 1)
            nc.vector.tensor_scalar(start_of[:, 0, :], bank[6][0:HI, 0:P], -float(CENTRE), None, ALU.add
                                    ).then_inc(s["start0"], 1)
            dve.wait_ge(s["src_row_in"], 16)
            src_tiles = src_row[:, :].rearrange("p (e t) -> p t e", t=RT)
            for g in range(RT // 4):
                dve.wait_ge(s["tile_mm"], g + 1)
                for k in range(4):
                    t = 4 * g + k
                    if t == 0:
                        dve.wait_ge(s["start0"], 1)
                    else:
                        dve.wait_ge(s["chained"], t)
                    nc.vector.tensor_tensor(start_of[:, t + 1, :], bank[g % 2][0:HI, P * k:P * k + P],
                                            start_of[:, t, :].bitcast(F32), ALU.add).then_inc(s["chained"], 1)
                for k in range(4):
                    t = 4 * g + k
                    need(dve, "within_done", t - 3)
                    nc.vector.scalar_tensor_tensor(
                        out=scrap[:, 0, k, 0:RP], in0=src_tiles[:, t, :], scalar=src_f[:, t:t + 1],
                        in1=earlier[0:RP, 0:RP], op0=ALU.is_equal, op1=ALU.mult,
                        accum_out=within[:, t:t + 1]).then_inc(s["within_done"], 1)
                for k in range(4):
                    t = 4 * g + k
                    dve.wait_ge(s["find_mm"], g + 1)
                    need(dve, "found_done", t - 3)
                    nc.vector.scalar_tensor_tensor(
                        out=scrap[:, 1, k, :], in0=bank[3 + g % 2][0:RP, P * k:P * k + P], scalar=1.0,
                        in1=is_lo[:, t, :], op0=ALU.mult, op1=ALU.mult,
                        accum_out=found[:, t:t + 1]).then_inc(s["found_done"], 1)
            dve.wait_ge(s["found_done"], RT)
            dve.wait_ge(s["within_done"], RT)
            nc.vector.scalar_tensor_tensor(out=pos_int[:, 0, :], in0=found[:, :], scalar=float(CENTRE),
                                           in1=within[:, :], op0=ALU.add, op1=ALU.add
                                           ).then_inc(s["rank_chain"], 1)
            dve.wait_ge(s["rank_chain"], 1)
            nc.vector.tensor_scalar(pos_int[:, 1, :], pos_int[:, 0, :], 7, None, ALU.logical_shift_right
                                    ).then_inc(s["rank_chain"], 1)
            nc.vector.tensor_scalar(pos_int[:, 2, :], pos_int[:, 0, :], P - 1, None, ALU.bitwise_and
                                    ).then_inc(s["rank_chain"], 1)
            dve.wait_ge(s["rank_chain"], 3)
            nc.vector.tensor_copy(pos_part[:, :, :], pos_int[:, 1:3, :]).then_inc(s["rank_chain"], 1)
            dve.wait_ge(s["rank_chain"], 4)
            for g in range(RT // 8):
                t = slice(8 * g, 8 * g + 8)
                need(dve, "index_mm", g)
                nc.vector.tensor_tensor(is_slot[:, :, :], iota_f[0:RP, :].unsqueeze(1).broadcast_to([RP, 8, P]),
                                        pos_part[:, 1, t].unsqueeze(2).broadcast_to([RP, 8, P]), ALU.is_equal)
                nc.vector.tensor_tensor(is_tile[:, :, :],
                                        iota_f[0:RP, 0:TILES].unsqueeze(1).broadcast_to([RP, 8, TILES]),
                                        pos_part[:, 0, t].unsqueeze(2).broadcast_to([RP, 8, TILES]),
                                        ALU.is_equal).then_inc(s["spread_used"], 1)
                dve.wait_ge(s["spread_used"], g + 1)
                nc.vector.tensor_tensor(spread[:, :, :, :],
                                        is_tile[:, :, :].unsqueeze(2).broadcast_to([RP, 8, VALS, TILES]),
                                        vals[:, t, :].unsqueeze(3).broadcast_to([RP, 8, VALS, TILES]),
                                        ALU.mult).then_inc(s["spread_ready"], 1)
            dve.wait_ge(s["index_mm"], RT // 8)
            nc.vector.tensor_copy(sorted_parts[:, :, :].rearrange("p v a -> p (v a)"),
                                  bank[6][:, 0:VALS * TILES]).then_inc(s["index_chain"], 1)
            dve.wait_ge(s["index_chain"], 1)
            for v, target in ((0, gather_index[:, 0, :]), (1, gather_index[:, 1, :]),
                              (2, src_sorted[:, 1:TILES + 1])):
                nc.vector.scalar_tensor_tensor(out=target, in0=sorted_parts[:, 2 * v, :], scalar=float(P),
                                               in1=sorted_parts[:, 2 * v + 1, :], op0=ALU.mult, op1=ALU.add
                                               ).then_inc(s["index_chain"], 1)
            dve.wait_ge(s["index_chain"], 4)
            nc.vector.tensor_tensor(src_sorted[:, TILES:TILES + 1], src_sorted[:, TILES:TILES + 1],
                                    pad_far[:, :], ALU.add).then_inc(s["src_sorted_ready"], 1)
            dve.wait_ge(s["src_sorted_ready"], 1)
            nc.vector.tensor_scalar(gather_index[:, 2, :], src_sorted[:, 1:TILES + 1], float(N - 1), None,
                                    ALU.min).then_inc(s["index_chain"], 1)
            dve.wait_ge(s["shift_mm"], 2)
            nc.vector.tensor_tensor(same_as_next[:, :], bank[7][:, 0:TILES], src_sorted[:, 1:TILES + 1],
                                    ALU.is_equal).then_inc(s["index_chain"], 1)
            nc.vector.tensor_tensor(same_as_before[:, :], bank[2][:, 0:TILES], src_sorted[:, 1:TILES + 1],
                                    ALU.is_equal).then_inc(s["index_chain"], 1)
            dve.wait_ge(s["row_mm"], 1)
            dve.wait_ge(s["bn2_halved"], 1)
            nc.vector.scalar_tensor_tensor(out=row_half[:, :], in0=bank[5][:, :], scalar=0.5,
                                           in1=bn2_half[:, :], op0=ALU.mult, op1=ALU.add
                                           ).then_inc(s["row_ready"], 1)
            dve.wait_ge(s["index_chain"], 7)
            nc.vector.scalar_tensor_tensor(out=store_index[:, :], in0=same_as_next[:, :], scalar=float(FAR),
                                           in1=src_sorted[:, 1:TILES + 1], op0=ALU.mult, op1=ALU.add
                                           ).then_inc(s["index_ready"], 1)

            def low(target, whole, high, name):
                nc.vector.tensor_tensor(target, whole, high.bitcast(F32), ALU.subtract).then_inc(s[name], 1)

            def split_attr(m):
                dve.wait_ge(s["attr_T_hi_ready"], m + 1)
                low(attr_T_lo[:, :], bank[4][:, :], attr_T_hi[:, :], "attr_T_lo_ready")

            def hidden_low(m):
                for c in range(C):
                    dve.wait_ge(s["h_silu"], C * m + c + 1)
                    low(h_lo[:, c, :], silu[:, c % 2, :], h_hi[:, c, :], "h_lo_ready")

            def agg_low(m, c):
                dve.wait_ge(s["agg_hi_ready"], C * m + c + 1)
                low(agg_lo[:, c, :], agg_T[:, c % 2, :], agg_hi[:, c, :], "agg_lo_ready")

            def base_add(m, i, b, half, k, name):
                n = base_rows(m, half, k)
                if k == 0:
                    dve.wait_ge(base_in[b][half], 16 * (i + 1) + (16 if base_rows(m, half, J - 1) < P and n == P
                                                                  and isinstance(m, int) else 0))
                if n:
                    t = base[0:n, b, half, k, :]
                    nc.vector.tensor_tensor(t, t, row_half[0:n, :], ALU.add).then_inc(s[name], 1)

            def moments(m, which, k, n, rows, stat, aggr):
                if k == 0:
                    need(dve, "moments_chain", moments_made(which, m - 1))
                nc.vector.bn_stats(stats[0:n, which, k, :], rows).then_inc(s[stat], 1)
                need(dve, stat, J * m + k + 1, True)
                nc.vector.bn_aggr(mean_var[0:n, which, k, :], stats[0:n, which, k, :]).then_inc(s[aggr], 1)

            def base_moments(m, b, half, k, added, which, stat, aggr):
                n = base_rows(m, half, k)
                if n:
                    dve.wait_ge(s[added], J * m + k + 1)
                    moments(m, which, k, n, base[0:n, b, half, k, :], stat, aggr)

            dve.wait_ge(s["be2_in"], 16)
            split_attr(0)
            hidden_low(0)

            def step(m, i, b):
                for c in range(C):
                    dve.wait_ge(s["ef_mm"], C * m + c + 1)
                    dve.wait_ge(s["xd_T_ready"], C * m + c + 1)
                    nc.vector.scalar_tensor_tensor(out=msg_T[:, c % 2, :], in0=bank[c][:, :],
                                                   scalar=be2_col[:, c:c + 1], in1=xd_T[:, c, :],
                                                   op0=ALU.add, op1=ALU.mult).then_inc(s["msg_ready"], 1)
                    if c == 0:
                        dve.wait_ge(s["mask_mm"], m + 1)
                        need(dve, "u_mm", C * m)
                        need(dve, "carried", C * m)
                    else:
                        agg_low(m, c - 1)
                    dve.wait_ge(s["msg_ready"], C * m + c + 1)
                    nc.vector.tensor_tensor_scan(agg_T[:, c % 2, :], bank[7][:, :], msg_T[:, c % 2, :],
                                                 carry[:, c:c + 1], ALU.mult, ALU.add
                                                 ).then_inc(s["scan_done"], 1)
                    base_add(m, i, b, 0, c, "base_added_a")
                    dve.wait_ge(s["scan_done"], C * m + c + 1)
                    nc.vector.tensor_copy(carry[:, c:c + 1], agg_T[:, c % 2, M - 1:M]).then_inc(s["carried"], 1)
                agg_low(m, C - 1)
                if not is_last(m):
                    split_attr(m + 1)
                    hidden_low(m + 1)
                for c in range(C):
                    base_moments(m, b, 0, c, "base_added_a", HALF_A, "dve_stats_a", "aggr_a")
                    base_add(m, i, b, 1, c, "base_added_b")
                    dve.wait_ge(s["u_silu"], C * m + c + 1)
                    low(u_lo[:, c, :], silu[:, c % 2, :], u_hi[:, c, :], "u_lo_ready")
                for j in range(J):
                    base_moments(m, b, 1, j, "base_added_b", HALF_B, "dve_stats_b", "aggr_b")
                    dve.wait_ge(s["y_mm"], C * m + j + 1)
                    if j == 0:
                        dve.wait_ge(s["xs_biased"], J * (m + 1))
                        need(dve, "out_stored", 16 * J * m)
                    nc.vector.scalar_tensor_tensor(out=z[:, j, :], in0=xs[:, j, :], scalar=2.0,
                                                   in1=bank[j][:, :], op0=ALU.mult, op1=ALU.add
                                                   ).then_inc(s["z_ready"], 1)
                    dve.wait_ge(s["z_ready"], J * m + j + 1)
                    moments(m, OUT, j, P, z[:, j, :], "dve_stats_out", "aggr_out")

            steps(dve, step)


POOL_CONSTS = 24


_INS = ["x", "src", "dst", "edge_attr_128", "L0_gnn_We1", "L0_gnn_be1", "L0_gnn_We2", "L0_gnn_be2",
        "L0_gnn_Wn1", "L0_gnn_bn1", "L0_gnn_Wn2", "L0_gnn_bn2"]


def kernel(**inputs):
    import numpy as np
    import concourse.bacc as bacc
    from concourse.bass_utils import run_bass_kernel_spmd

    nc = bacc.Bacc("TRN2", target_bir_lowering=False, num_devices=1)
    arrays, args = {}, []
    for name in _INS:
        a = np.ascontiguousarray(inputs[name])
        arrays[f"in_{name}"] = a
        args.append(nc.dram_tensor(f"in_{name}", a.shape, mybir.dt.from_np(a.dtype), kind="ExternalInput").ap())
    shape = arrays["in_x"].shape
    args.append(nc.dram_tensor("out_rows", shape, F32, kind="ExternalOutput").ap())
    gnn_kernel(nc, *args)
    r = run_bass_kernel_spmd(nc, [arrays], core_ids=[0])
    return r.results[0]["out_rows"]
```

```python
from contextlib import ExitStack

import concourse.bass as bass
from concourse import mybir

F32 = mybir.dt.float32
F32R = mybir.dt.float32r
BF16 = mybir.dt.bfloat16
F16 = mybir.dt.float16
I32 = mybir.dt.int32
ALU = mybir.AluOpType
ACT = mybir.ActivationFunctionType

P = 128
EPS = 1e-5
FAR = 16384


def gnn_kernel(nc, x, src, dst, edge_attr, we1, be1, we2, be2, wn1, bn1, wn2, bn2, out):
    N, H = x.shape
    E, R = edge_attr.shape
    assert R == P and H % P == 0 and H <= 512 and N < FAR
    C = H // P
    J = 4
    M = J * P
    MACROS = -(-E // M)
    TILES = MACROS * J
    PAIRS = MACROS // 2
    assert MACROS % 2 == 0 and PAIRS >= 3
    NT = -(-N // P)
    assert 2 * J * (MACROS - 1) < NT <= 2 * J * MACROS and NT <= TILES * 2
    RT = 40
    RP = E // RT
    assert RP * RT == E and RP <= P and RT % 8 == 0
    GROUPS = RT // 4
    ROUNDS = RT // 8
    HI = 80
    assert NT <= HI
    CENTRE = E // 2
    assert CENTRE < 4096
    VALS = 4
    LOW = 4096
    assert N <= 4 * LOW and E <= 4 * LOW

    with ExitStack() as ctx:
        def sb(name, shape, dt=F32, stack=ctx):
            return stack.enter_context(nc.sbuf_tensor(name, shape, dt))

        def sem(name):
            return ctx.enter_context(nc.semaphore(name))

        bank = [ctx.enter_context(nc.psum_tensor(f"bank{n}", [P, 512], F32)) for n in range(8)]

        we1_hi, we1_lo = sb("we1_hi", [P, H], F32R), sb("we1_lo", [P, H], F32R)
        we2_hi, we2_lo = sb("we2_hi", [P, C, H], F32R), sb("we2_lo", [P, C, H], F32R)
        wn1_hi, wn1_lo = sb("wn1_hi", [P, C, H], F32R), sb("wn1_lo", [P, C, H], F32R)
        wn2_hi, wn2_lo = sb("wn2_hi", [P, C, H], F32R), sb("wn2_lo", [P, C, H], F32R)
        be1_col, be2_col, bn1_col = sb("be1_col", [P, C]), sb("be2_col", [P, C]), sb("bn1_col", [P, C])
        bn2_half = sb("bn2_half", [P, H])
        row_half = sb("row_half", [P, H])
        ident, ident_bf = sb("ident", [P, P]), sb("ident_bf", [P, P], BF16)
        minus_half = sb("minus_half", [P, 2 * J])
        gather_index = sb("gather_index", [P, 3, TILES], I32)
        store_index = sb("store_index", [P, TILES], I32)
        base_index = sb("base_index", [P, 2 * TILES], I32)
        same_as_before = sb("same_as_before", [P, TILES], BF16)
        carry = sb("carry", [P, C])
        z = sb("z", [P, J, H])

        with ExitStack() as loading:
            we1_raw = sb("we1_raw", [P, H], stack=loading)
            we2_raw, wn1_raw, wn2_raw = (sb(f"{w}_raw", [P, C, H], stack=loading) for w in ("we2", "wn1", "wn2"))
        base = sb("base", [P, 2, 2, J, H])

        with ExitStack() as early:
            def eb(name, shape, dt=F32):
                return sb(name, shape, dt, early)

            is_hi_T = eb("is_hi_T", [HI, RT, P], F32R)
            is_hi_T_bf = eb("is_hi_T_bf", [HI, RT, RP], BF16)
            edge_int = eb("edge_int", [RP, 3, RT], I32)
            node_part = eb("node_part", [RP, 2, RT], I32)
            low_int, high_int = eb("low_int", [RP, 3, RT], I32), eb("high_int", [RP, 3, RT], I32)
            high_two = eb("high_two", [RP, RT])
            vals = eb("vals", [RP, RT, VALS], F16)
            iota_int = eb("iota_int", [P, P], I32)
            node_int = eb("node_int", [P, 2 * TILES], I32)
            later = eb("later", [P, P])
            take_next, wrap_next = eb("take_next", [P, P]), eb("wrap_next", [P, P])
            take_prev, wrap_prev = eb("take_prev", [P, P]), eb("wrap_prev", [P, P])
            pad_far = eb("pad_far", [P, 1])
            is_lo = eb("is_lo", [RP, RT, P], BF16)
            is_hi = eb("is_hi", [RP, RT, HI], BF16)
            counts = eb("counts", [HI, GROUPS, P], F16)
            up_to = eb("up_to", [HI, P])
            below = eb("below", [HI, 1])
            start = eb("start", [HI, P])
            ones, zero_col = eb("ones", [HI, P]), eb("zero_col", [HI, 1])
            silu_of_zero = eb("silu_of_zero", [HI, 1])
            ident_16 = eb("ident_16", [HI, HI], F16)
            total = eb("total", [HI, P])
            group_start = eb("group_start", [HI, GROUPS, P], F32R)
            start_of = eb("start_of", [HI, RT, P], F32R)
            ident_r = eb("ident_r", [HI, HI], F32R)
            total_T = eb("total_T", [P, HI])
            touched = eb("touched", [P, HI])
            found = eb("found", [RP, RT])
            same_hi = eb("same_hi", [RP, RT, RP], BF16)
            scrap = eb("scrap", [RP, 4, P])
            pos_int = eb("pos_int", [RP, 3, RT], I32)
            is_slot = eb("is_slot", [RP, 2, 8, P], F16)
            is_tile = eb("is_tile", [RP, 2, 8, TILES], F16)
            spread = eb("spread", [RP, 2, 8, VALS, TILES], F16)
            sorted_low = eb("sorted_low", [P, 3, TILES], I32)
            sorted_high = eb("sorted_high", [P, TILES], I32)
            sorted_top = eb("sorted_top", [P, 3, TILES], I32)
            src_sorted = eb("src_sorted", [P, TILES + 2])
            same_as_next = eb("same_as_next", [P, TILES])
            bn2_row = eb("bn2_row", [P, H])
            mid = eb("mid", [P, C])
            mid_hi, mid_lo = eb("mid_hi", [P, C], F32R), eb("mid_lo", [P, C], F32R)
        attr = sb("attr", [P, 2, J, R])
        xd = sb("xd", [P, 2, J, H])
        xs = sb("xs", [P, J, H])
        attr_T_hi, attr_T_lo = sb("attr_T_hi", [P, M], F32R), sb("attr_T_lo", [P, M], F32R)
        h_hi, h_lo = sb("h_hi", [P, C, M], F32R), sb("h_lo", [P, C, M], F32R)
        u_hi, u_lo = sb("u_hi", [P, C, M], F32R), sb("u_lo", [P, C, M], F32R)
        agg_hi, agg_lo = sb("agg_hi", [P, C, M], F32R), sb("agg_lo", [P, C, M], F32R)
        xd_T = sb("xd_T", [P, C, M])
        msg_T = sb("msg_T", [P, 2, M])
        agg_T = sb("agg_T", [P, 2, M])
        silu = sb("silu", [P, 2, M])
        gather_now = sb("gather_now", [P, 2, 2, J], I32)
        own_now = sb("own_now", [P, 2, J], I32)
        store_now = sb("store_now", [P, 2, J], I32)
        base_now = sb("base_now", [P, 2, 2, J], I32)
        stats = sb("stats", [P, 3, J, 6])
        mean_var = sb("mean_var", [P, 3, J, 2])
        var_eps, rstd = sb("var_eps", [P, 3, J]), sb("rstd", [P, 3, J])
        shift = sb("shift", [P, 3, J])
        HALF_A, HALF_B, OUT = 0, 1, 2

        s = {name: sem(name) for name in (
            "src_in dst_in be1_in be2_in bn1_in bn2_in we1_in we2_in wn1_in wn2_in "
            "numbers_ready pool_const we_hi wn1_hi wn2_hi we_lo wn1_lo wn2_lo bn2_halved mid_split mid_low row_mm row_ready "
            "parts one_hots vals_ready counts_mm counts_ready counted_mm up_to_ready below_mm start_chain total_copied total_T_mm total_T_ready "
            "start_ready consts_r_ready tile_start_mm tile_start_ready hi_T_mm hi_T_ready hi_T_bf_pool hi_T_bf_dve "
            "is_slot_ready find_mm found_done same_hi_mm same_hi_copied same_hi_ready rank_chain is_tile_ready spread_ready index_mm "
            "index_chain edges_ready src_sorted_ready shift_mm index_ready base_index_ready "
            "attr_T_mm attr_T_hi_ready attr_T_lo_ready h_mm h_silu h_lo_ready ef_mm msg_ready scan_done carried "
            "agg_hi_ready agg_lo_ready u_mm u_silu u_lo_ready xd_T_mm xd_T_ready mask_mm y_mm z_ready "
            "dve_stats_out dve_stats_a dve_stats_b base_added_a base_added_b aggr_out aggr_a aggr_b "
            "rows_out rows_a rows_b var_ready rstd_ready shift_ready copied_gather copied_own copied_store copied_base "
            "xs_biased xs_in out_stored passed"
        ).split()}
        attr_in = [sem(f"attr_in{b}") for b in range(2)]
        xd_in = [sem(f"xd_in{b}") for b in range(2)]
        base_in = [[sem(f"base_in{b}{h}") for h in range(2)] for b in range(2)]
        base_stored = [[sem(f"base_stored{b}{h}") for h in range(2)] for b in range(2)]

        def need(eng, name, count, alone=False):
            if isinstance(count, int) and count <= 0:
                return
            eng.wait_ge(s[name] if isinstance(name, str) else name, count)
            if alone and not isinstance(count, int):
                eng.sem_inc(s["passed"], 1)

        def steps(eng, step):
            for b in range(2):
                step(b, 0, b)
            with eng.Fori(1, PAIRS - 1) as i:
                for b in range(2):
                    step(2 * i + b, i, b)
            for b in range(2):
                step(MACROS - 2 + b, PAIRS - 1, b)

        def is_last(m):
            return isinstance(m, int) and m == MACROS - 1

        EARLY = 6
        assert 6 <= EARLY and GROUPS - EARLY <= 4

        def counts_bank(g):
            return bank[(4, 6)[g % 2]][0:HI, 0:P]

        def counted(g):
            at = (g - 1) % 4
            return bank[(0, 1, 3)[(g - 1) // 4]][0:HI, P * at:P * at + P]

        POOL_COPIES = 4

        def same_hi_bank(g):
            return bank[(2, 7)[g % 2]][0:RP, 0:4 * RP].rearrange("p (k e) -> p k e", k=4)

        def base_rows(m, half, k):
            if not isinstance(m, int):
                return P
            return max(0, min(P, N - ((2 * m + half) * J + k) * P))

        def hi_T_bank(g):
            return bank[(2, 7)[g % 2]][0:HI, 0:256].bitcast(BF16).rearrange("p (k e) -> p k e", k=4)[:, :, 0:RP]

        def moments_made(which, m):
            return 2 * m + (1 if which == HALF_A else 2)

        def together(t, which):
            return t[:, 0:1, :] if which == HALF_A else t[:, 1:3, :]

        block = ctx.enter_context(nc.Block())

        @block.sync
        def _(sp):
            sp.dma_start(edge_int[:, 2, :], src.rearrange("(p t) -> p t", t=RT)).then_inc(s["src_in"], 16)
            sp.dma_start(edge_int[:, 1, :], dst.rearrange("(p t) -> p t", t=RT)).then_inc(s["dst_in"], 16)
            sp.dma_start(we1_raw[:, :], we1).then_inc(s["we1_in"], 16)
            for w, r, name in ((we2, we2_raw, "we2_in"), (wn2, wn2_raw, "wn2_in"), (wn1, wn1_raw, "wn1_in")):
                sp.dma_start(r[:, :, :], w.rearrange("(c p) n -> p c n", p=P)).then_inc(s[name], 16)
            sp.wait_ge(s["wn2_lo"], C)
            sp.wait_ge(s["we_lo"], 1 + C)
            sp.wait_ge(s["wn1_lo"], C)
            sp.wait_ge(s["xd_T_mm"], 1)

            def step(m, i, b):
                for half in range(2):
                    need(sp, base_stored[b][half], 64 * i)
                    first = (2 * m + half) * J * P
                    full = sum(base_rows(m, half, k) == P for k in range(J))
                    sp.dma_start(base[:, b, half, 0:full, :],
                                 x[bass.ds(first, full * P), :].rearrange("(k p) h -> p k h", p=P)
                                 ).then_inc(base_in[b][half], 16)
                    if full < J and base_rows(m, half, full):
                        n = base_rows(m, half, full)
                        sp.dma_start(base[0:n, b, half, full, :], x[N - n:N, :]).then_inc(base_in[b][half], 16)

            steps(sp, step)

        @block.gpsimd
        def _(pool):
            consts = [0]

            def const(ins):
                ins.then_inc(s["pool_const"], 1)
                consts[0] += 1

            nc.gpsimd.iota(iota_int[:, :], [[1, P]], base=0, channel_multiplier=0
                           ).then_inc(s["numbers_ready"], 1)
            nc.gpsimd.iota(edge_int[:, 0, :], [[1, RT]], base=0, channel_multiplier=RT
                           ).then_inc(s["numbers_ready"], 1)
            for t in (ident_bf, ident, take_next, wrap_next, take_prev, wrap_prev):
                const(nc.gpsimd.memset(t[:, :], 0.0))
            const(nc.gpsimd.memset(later[:, :], 1.0))
            const(nc.gpsimd.memset(ones[:, :], 1.0))
            const(nc.gpsimd.memset(zero_col[:, :], 0.0))
            const(nc.gpsimd.memset(pad_far[:, :], float(FAR)))
            const(nc.gpsimd.memset(minus_half[:, :], -0.5))
            const(nc.gpsimd.memset(carry[:, :], 0.0))
            const(nc.gpsimd.memset(src_sorted[:, :], -1.0))
            const(nc.gpsimd.iota(node_int[:, :], [[P, 2 * TILES]], base=0, channel_multiplier=1))
            pool.wait_ge(s["pool_const"], consts[0])
            for t, at in ((ident_bf, 0), (ident, 0), (take_next, -1), (wrap_next, P - 1), (take_prev, 1),
                          (wrap_prev, -(P - 1))):
                const(nc.gpsimd.affine_select(out=t[:, :], in_=t[:, :], compare_op=ALU.not_equal, fill=1.0,
                                              base=at, pattern=[[-1, P]], channel_multiplier=1))
            const(nc.gpsimd.affine_select(out=later[:, :], in_=later[:, :], compare_op=ALU.is_gt, fill=0.0,
                                          base=0, pattern=[[1, P]], channel_multiplier=-1))
            const(nc.gpsimd.affine_select(out=pad_far[:, :], in_=pad_far[:, :], compare_op=ALU.is_ge, fill=0.0,
                                          base=-(E - (TILES - 1) * P), pattern=[[0, 1]], channel_multiplier=1))
            assert consts[0] == POOL_CONSTS

            for g in range(POOL_COPIES):
                t = slice(4 * g, 4 * g + 4)
                pool.wait_ge(s["hi_T_ready"], g + 1)
                nc.gpsimd.tensor_copy(is_hi_T_bf[:, t, :], is_hi_T[:, t, 0:RP].bitcast(F32)
                                      ).then_inc(s["hi_T_bf_pool"], 1)
            for g in range(GROUPS):
                pool.wait_ge(s["same_hi_copied"], g + 1)
                pairs = same_hi[:, 4 * g:4 * g + 4, :]
                nc.gpsimd.affine_select(out=pairs, in_=pairs, compare_op=ALU.is_gt, fill=0.0, base=0,
                                        pattern=[[0, 4], [1, RP]], channel_multiplier=-1
                                        ).then_inc(s["same_hi_ready"], 1)
                c = g - (GROUPS - C)
                if c >= 0:
                    pool.wait_ge(s["wn2_hi"], c + 1)
                    nc.gpsimd.tensor_tensor(wn2_lo[:, c, :], wn2_raw[:, c, :], wn2_hi[:, c, :].bitcast(F32),
                                            ALU.subtract).then_inc(s["wn2_lo"], 1)
            for q in range(ROUNDS):
                pool.wait_ge(s["vals_ready"], 5)
                pool.wait_ge(s["is_tile_ready"], q + 1)
                need(pool, "index_mm", q - 1)
                nc.gpsimd.tensor_tensor(spread[:, q % 2, :, :, :],
                                        is_tile[:, q % 2, :, :].unsqueeze(2).broadcast_to([RP, 8, VALS, TILES]),
                                        vals[:, 8 * q:8 * q + 8, :].unsqueeze(3).broadcast_to([RP, 8, VALS, TILES]),
                                        ALU.mult).then_inc(s["spread_ready"], 1)

            pool.wait_ge(s["edges_ready"], 1)

            def gather_attr(m, i, b):
                need(pool, "attr_T_mm", m - 1, True)
                need(pool, "xd_T_mm", C * (m - 1), True)
                nc.gpsimd.tensor_copy(gather_now[:, b, :, :], gather_index[:, 0:2, bass.ds(m * J, J)]
                                      ).then_inc(s["copied_gather"], 1)
                need(pool, "copied_gather", m + 1, True)
                for j in range(J):
                    pool.indirect_dma_start(
                        out=attr[:, b, j, :], out_offset=None, in_=edge_attr,
                        in_offset=bass.IndirectOffsetOnAxis(ap=gather_now[:, b, 0, j:j + 1], axis=0),
                    ).then_inc(attr_in[b], 16)

            def gather_dst(m, i, b):
                for j in range(J):
                    pool.indirect_dma_start(
                        out=xd[:, b, j, :], out_offset=None, in_=x,
                        in_offset=bass.IndirectOffsetOnAxis(ap=gather_now[:, b, 1, j:j + 1], axis=0),
                    ).then_inc(xd_in[b], 16)

            def base_add(m, i, b):
                pool.wait_ge(s["row_ready"], 1)
                need(pool, base_in[b][0], 16 * (i + 1), True)
                for k in range(J):
                    assert base_rows(m, 0, k) == P
                    t = base[:, b, 0, k, :]
                    nc.gpsimd.tensor_tensor(t, t, row_half[:, :], ALU.add).then_inc(s["base_added_a"], 1)

            def rstd_of(which, m):
                need(pool, "var_ready", 3 * m + (1 if which == HALF_A else 3), True)
                for rows in (("rows_a",) if which == HALF_A else ("rows_b", "rows_out")):
                    need(pool, rows, J * m, True)
                v = together(var_eps, which)
                n = v.shape[1]
                nc.gpsimd.tensor_tensor(together(rstd, which), v,
                                        minus_half[:, 0:n * J].rearrange("p (g k) -> p g k", g=n),
                                        ALU.pow).then_inc(s["rstd_ready"], 1)

            def store_base(m, i, b, half, rows):
                for k in range(J):
                    n = base_rows(m, half, k)
                    if n:
                        need(pool, rows, J * m + k + 1, True)
                        pool.indirect_dma_start(
                            out=out, in_=base[0:n, b, half, k, :], in_offset=None,
                            out_offset=bass.IndirectOffsetOnAxis(ap=base_now[0:n, b, half, k:k + 1], axis=0),
                            bounds_check=N - 1, oob_is_err=False).then_inc(base_stored[b][half], 16)

            def store_sorted(m, i, b):
                need(pool, "out_stored", 16 * J * (m - 1), True)
                nc.gpsimd.tensor_copy(store_now[:, b, :], store_index[:, bass.ds(m * J, J)]
                                      ).then_inc(s["copied_store"], 1)
                need(pool, "copied_store", m + 1, True)
                for j in range(J):
                    need(pool, "rows_out", J * m + j + 1, True)
                    pool.indirect_dma_start(
                        out=out, in_=z[:, j, :], in_offset=None,
                        out_offset=bass.IndirectOffsetOnAxis(ap=store_now[:, b, j:j + 1], axis=0),
                        bounds_check=N - 1, oob_is_err=False).then_inc(s["out_stored"], 16)

            def base_indices(m, i, b):
                for half in range(2):
                    need(pool, base_stored[b][half], 16 * J * i, True)
                nc.gpsimd.tensor_copy(base_now[:, b, :, :], base_index[:, bass.ds(m * 2 * J, 2 * J)]
                                      .rearrange("p (h k) -> p h k", h=2)).then_inc(s["copied_base"], 1)
                need(pool, "copied_base", m + 1, True)

            gather_attr(0, 0, 0)
            gather_dst(0, 0, 0)
            pool.wait_ge(s["index_ready"], 1)
            gather_attr(1, 0, 1)
            gather_dst(1, 0, 1)

            def step(m, i, b):
                first, more = isinstance(m, int) and m == 0, not (isinstance(m, int) and m >= MACROS - 2)
                before = (m - 1, i if b else i - 1, 1 - b)
                if not first:
                    rstd_of(HALF_B, m - 1)
                need(pool, "z_ready", J * m, True)
                nc.gpsimd.tensor_copy(own_now[:, b, :], gather_index[:, 2, bass.ds(m * J, J)]
                                      ).then_inc(s["copied_own"], 1)
                need(pool, "copied_own", m + 1, True)
                for j in range(J):
                    pool.indirect_dma_start(
                        out=xs[:, j, :], out_offset=None, in_=x,
                        in_offset=bass.IndirectOffsetOnAxis(ap=own_now[:, b, j:j + 1], axis=0),
                    ).then_inc(s["xs_in"], 16)
                if not first:
                    base_indices(*before)
                    store_base(*before, 0, "rows_a")
                if more:
                    gather_attr(m + 2, i + 1, b)
                if not first:
                    store_sorted(*before)
                if more:
                    gather_dst(m + 2, i + 1, b)
                if not first:
                    store_base(*before, 1, "rows_b")
                if first:
                    base_add(m, i, b)
                rstd_of(HALF_A, m)
                if not is_last(m):
                    base_add(m + 1, i if b == 0 else i + 1, 1 - b)

            steps(pool, step)
            last = (MACROS - 1, PAIRS - 1, 1)
            rstd_of(HALF_B, MACROS - 1)
            base_indices(*last)
            store_base(*last, 0, "rows_a")
            store_base(*last, 1, "rows_b")
            store_sorted(*last)
            need(pool, "out_stored", 16 * TILES, True)
            for b in range(2):
                for half in range(2):
                    tiles = sum(base_rows(m, half, k) > 0 for m in range(b, MACROS, 2) for k in range(J))
                    pool.wait_ge(base_stored[b][half], 16 * tiles)

        @block.scalar
        def _(act):
            act.dma_start(bn2_row[:, :], bn2.rearrange("(o h) -> o h", o=1).broadcast_to([P, H])
                          ).then_inc(s["bn2_in"], 16)
            for v, t, name in ((be1, be1_col, "be1_in"), (be2, be2_col, "be2_in"), (bn1, bn1_col, "bn1_in")):
                act.dma_start(t[:, :], v.rearrange("(c p) -> p c", p=P), allow_slow_non_contiguous=True
                              ).then_inc(s[name], 16)
            act.wait_ge(s["pool_const"], POOL_CONSTS)
            nc.scalar.activation(silu_of_zero[:, :], zero_col[:, :], ACT.Silu)
            nc.scalar.activation(ident_r[:, :], ident[0:HI, 0:HI], ACT.Copy).then_inc(s["consts_r_ready"], 1)
            nc.scalar.activation(ident_16[:, :], ident[0:HI, 0:HI], ACT.Copy).then_inc(s["consts_r_ready"], 1)
            for g in range(GROUPS):
                act.wait_ge(s["counts_mm"], g + 1)
                nc.scalar.activation(counts[:, g, :], counts_bank(g), ACT.Copy).then_inc(s["counts_ready"], 1)
                act.wait_ge(s["hi_T_mm"], g + 1)
                nc.scalar.activation(is_hi_T[:, 4 * g:4 * g + 4, 0:RP],
                                     hi_T_bank(g), ACT.Copy).then_inc(s["hi_T_ready"], 1)
            highs = ([("wn2_in", wn2_hi, wn2_raw, c, "wn2_hi") for c in range(C)]
                     + [("we1_in", we1_hi, we1_raw, None, "we_hi")]
                     + [("we2_in", we2_hi, we2_raw, c, "we_hi") for c in range(C)]
                     + [("wn1_in", wn1_hi, wn1_raw, c, "wn1_hi") for c in range(C)])

            def high(name, hi, raw, c, done):
                act.wait_ge(s[name], 16)
                hi, raw = (hi[:, :], raw[:, :]) if c is None else (hi[:, c, :], raw[:, c, :])
                nc.scalar.activation(hi, raw, ACT.Copy).then_inc(s[done], 1)

            def copy_same_hi(g):
                act.wait_ge(s["same_hi_mm"], g + 1)
                nc.scalar.activation(same_hi[:, 4 * g:4 * g + 4, :], same_hi_bank(g), ACT.Copy
                                     ).then_inc(s["same_hi_copied"], 1)

            for g in range(4):
                copy_same_hi(g)
            for g in range(GROUPS):
                act.wait_ge(s["tile_start_mm"], g + 1)
                nc.scalar.activation(start_of[:, 4 * g:4 * g + 4, :].rearrange("p k n -> p (k n)"),
                                     bank[g % 2][0:HI, :], ACT.Copy).then_inc(s["tile_start_ready"], 1)
                for ahead in ((4, 5) if g == 0 else (g + 5,)):
                    if ahead < GROUPS:
                        copy_same_hi(ahead)
                if g == 0:
                    act.wait_ge(s["total_T_mm"], 1)
                    nc.scalar.activation(total_T[:, :], bank[5][0:P, 0:HI], ACT.Copy).then_inc(s["total_T_ready"], 1)
                if g == 1:
                    act.wait_ge(s["bn1_in"], 16)
                    nc.scalar.activation(mid_hi[:, :], bn1_col[:, :], ACT.Silu)
                    nc.scalar.activation(mid[:, :], bn1_col[:, :], ACT.Silu).then_inc(s["mid_split"], 1)
                    act.wait_ge(s["bn2_in"], 16)
                    nc.scalar.activation(bn2_half[:, :], bn2_row[:, :], ACT.Copy, scale=0.5).then_inc(s["bn2_halved"], 1)
                high(*highs[g])
            for g in range(GROUPS, len(highs)):
                high(*highs[g])
            act.wait_ge(s["index_ready"], 1)

            def split_attr(m):
                act.wait_ge(s["attr_T_mm"], m + 1)
                need(act, "h_mm", C * m)
                nc.scalar.activation(attr_T_hi[:, :], bank[4][:, :], ACT.Copy).then_inc(s["attr_T_hi_ready"], 1)

            def hidden(m, c):
                act.wait_ge(s["h_mm"], C * m + c + 1)
                if c == 0:
                    need(act, "ef_mm", C * m)
                if c >= 2:
                    need(act, "h_lo_ready", C * m + c - 1)
                else:
                    need(act, "u_lo_ready", C * (m - 2) + c + 3)
                nc.scalar.activation(h_hi[:, c, :], bank[c][:, :], ACT.Silu, bias=be1_col[:, c:c + 1])
                nc.scalar.activation(silu[:, c % 2, :], bank[c][:, :], ACT.Silu, bias=be1_col[:, c:c + 1]
                                     ).then_inc(s["h_silu"], 1)

            def transposed_rows(m, chunks):
                for c in chunks:
                    act.wait_ge(s["xd_T_mm"], C * m + c + 1)
                    need(act, "msg_ready", C * (m - 1) + c + 1)
                    nc.scalar.activation(xd_T[:, c, :], bank[5 + c % 2][:, :], ACT.Copy
                                         ).then_inc(s["xd_T_ready"], 1)

            def norm_base(m, b, half, k, which, rows):
                n = base_rows(m, half, k)
                if n:
                    if k == 0:
                        act.wait_ge(s["shift_ready"], moments_made(which, m))
                    t = base[0:n, b, half, k, :]
                    nc.scalar.activation(t, t, ACT.Identity, bias=shift[0:n, which, k:k + 1],
                                         scale=rstd[0:n, which, k:k + 1]).then_inc(s[rows], 1)

            def norm_sorted(m, j):
                if j == 0:
                    act.wait_ge(s["shift_ready"], moments_made(OUT, m))
                nc.scalar.activation(z[:, j, :], z[:, j, :], ACT.Identity, bias=shift[:, OUT, j:j + 1],
                                     scale=rstd[:, OUT, j:j + 1]).then_inc(s["rows_out"], 1)

            act.wait_ge(s["be1_in"], 16)
            split_attr(0)
            for c in range(C):
                hidden(0, c)
            transposed_rows(0, range(C))

            def step(m, i, b):
                first = isinstance(m, int) and m == 0
                norms = [] if first else [(OUT, k) for k in range(J)] + [(HALF_B, k) for k in range(J)]

                def norm(n):
                    for kind, k in norms[0:n]:
                        if kind == OUT:
                            norm_sorted(m - 1, k)
                        else:
                            norm_base(m - 1, 1 - b, 1, k, HALF_B, "rows_b")
                    del norms[0:n]

                for c in range(C):
                    if c == C - 1 and not is_last(m):
                        hidden(m + 1, 0)
                    act.wait_ge(s["scan_done"], C * m + c + 1)
                    if c == 0:
                        need(act, "u_mm", C * m)
                    nc.scalar.activation(agg_hi[:, c, :], agg_T[:, c % 2, :], ACT.Copy
                                         ).then_inc(s["agg_hi_ready"], 1)
                    if c == 1 and not is_last(m):
                        split_attr(m + 1)
                    norm((0, 2, 1, 0)[c])
                for c in range(1, C):
                    if not is_last(m):
                        hidden(m + 1, c)
                    norm(2 if c < C - 1 else 1)
                for c in range(C):
                    act.wait_ge(s["u_mm"], C * m + c + 1)
                    if c == 0:
                        need(act, "y_mm", C * m)
                    if c >= 2:
                        need(act, "u_lo_ready", C * m + c - 1)
                    elif is_last(m):
                        need(act, "u_lo_ready", C * (m - 1) + c + 3)
                    else:
                        need(act, "h_lo_ready", C * (m + 1) + c + 3)
                    nc.scalar.activation(u_hi[:, c, :], bank[c][:, :], ACT.Silu, bias=bn1_col[:, c:c + 1])
                    nc.scalar.activation(silu[:, c % 2, :], bank[c][:, :], ACT.Silu, bias=bn1_col[:, c:c + 1]
                                         ).then_inc(s["u_silu"], 1)
                    if c >= C - 2 and not is_last(m):
                        transposed_rows(m + 1, range(0, 2) if c == C - 2 else range(2, C))
                for k in range(J):
                    norm_base(m, b, 0, k, HALF_A, "rows_a")

            steps(act, step)
            for j in range(J):
                norm_base(MACROS - 1, 1, 1, j, HALF_B, "rows_b")
                norm_sorted(MACROS - 1, j)

        def product(pe, target, lhs_hi, lhs_lo, rhs_hi, rhs_lo, start, stop):
            pe.matmul(target, lhs_lo, rhs_hi, start=start, stop=False)
            pe.matmul(target, lhs_hi, rhs_lo, start=False, stop=False)
            return pe.matmul(target, lhs_hi, rhs_hi, start=False, stop=stop)

        @block.tensor
        def _(pe):
            def add_counts(g):
                pe.wait_ge(s["counts_ready"], g + 1)
                for n, b in enumerate((0, 1, 3)):
                    first, last = max(g + 1, 4 * n + 1), min(4 * n + 4, GROUPS)
                    if first <= last:
                        k = last - first + 1
                        at = (first - 1) % 4
                        mm = pe.matmul(bank[b][0:HI, P * at:P * (at + k)].rearrange("p (k n) -> p k n", k=k),
                                       ident_16[:, :], counts[:, g, :].unsqueeze(1).broadcast_to([HI, k, P]),
                                       start=(g == 0), stop=(g + 1 == last))
                if g in (3, 7, GROUPS - 1):
                    mm.then_inc(s["counted_mm"], 1)

            pe.wait_ge(s["pool_const"], POOL_CONSTS)
            pe.wait_ge(s["consts_r_ready"], 2)
            for g in range(GROUPS):
                pe.wait_ge(s["one_hots"], 2 * (g // 2 + 1))
                need(pe, "counts_ready", g - 1)
                for t in range(4 * g, 4 * g + 4):
                    mm = pe.matmul(counts_bank(g), is_hi[:, t, :], is_lo[:, t, :], start=(t % 4 == 0),
                                   stop=(t % 4 == 3))
                mm.then_inc(s["counts_mm"], 1)
                need(pe, "hi_T_ready", g - 1)
                for k in range(4):
                    mm = pe.transpose(hi_T_bank(g)[:, k, :], is_hi[:, 4 * g + k, :], ident_bf[0:RP, 0:RP])
                mm.then_inc(s["hi_T_mm"], 1)
                if g:
                    add_counts(g - 1)
            add_counts(GROUPS - 1)

            def pairs(g):
                pe.wait_ge(s["hi_T_ready"], GROUPS)
                if g < POOL_COPIES:
                    pe.wait_ge(s["hi_T_bf_pool"], g + 1)
                else:
                    pe.wait_ge(s["hi_T_bf_dve"], g + 1 - POOL_COPIES)
                need(pe, "same_hi_copied", g - 1)
                for k in range(4):
                    t = 4 * g + k
                    mm = pe.matmul(same_hi_bank(g)[:, k, :], is_hi_T_bf[:, t, :], is_hi_T_bf[:, t, :], start=True,
                                   stop=True)
                mm.then_inc(s["same_hi_mm"], 1)

            pairs(0)
            pe.wait_ge(s["up_to_ready"], 1)
            pe.matmul(bank[4][0:HI, 0:1], later[0:HI, 0:HI], up_to[:, P - 1:P], start=True, stop=True
                      ).then_inc(s["below_mm"], 1)

            def tile_starts(g):
                need(pe, "tile_start_ready", g - 1)
                pe.wait_ge(s["start_ready"], max((g + 3) // 4 + 1, g % 2 + 2))
                places = bank[g % 2][0:HI, :].rearrange("p (k n) -> p k n", k=4)
                pe.matmul(places, ident_r[:, :], group_start[:, g, :].unsqueeze(1).broadcast_to([HI, 4, P]),
                          start=True, stop=False)
                for k in range(3):
                    mm = pe.matmul(places[:, k + 1:4, :], is_hi[:, 4 * g + k, :],
                                   is_lo[:, 4 * g + k, :].unsqueeze(1).broadcast_to([RP, 3 - k, P]),
                                   start=False, stop=(k == 2))
                mm.then_inc(s["tile_start_mm"], 1)

            def find(g):
                pe.wait_ge(s["tile_start_ready"], g + 1)
                pe.wait_ge(s["same_hi_ready"], g + 1)
                need(pe, "found_done", 4 * (g - 1))
                for k in range(4):
                    t = 4 * g + k
                    places = bank[(4, 6)[g % 2]][0:RP, P * k:P * k + P]
                    pe.matmul(places, is_hi_T[:, t, 0:RP], start_of[:, t, :], start=True, stop=False)
                    mm = pe.matmul(places, same_hi[:, t, :], is_lo[:, t, :], start=False, stop=True)
                mm.then_inc(s["find_mm"], 1)

            def index(q):
                pe.wait_ge(s["spread_ready"], q + 1)
                pe.wait_ge(s["is_slot_ready"], q + 1)
                if q == 0:
                    pe.wait_ge(s["total_T_ready"], 1)
                for k in range(8):
                    mm = pe.matmul(bank[5][:, 0:VALS * TILES], is_slot[:, q % 2, k, :],
                                   spread[:, q % 2, k, :, :].rearrange("p v a -> p (v a)"),
                                   start=(q == 0 and k == 0), stop=(q == ROUNDS - 1 and k == 7))
                mm.then_inc(s["index_mm"], 1)

            for g in range(1, EARLY):
                pairs(g)
            pe.wait_ge(s["total_copied"], 1)
            pe.transpose(bank[5][0:P, 0:HI], total[:, :], ident[0:HI, 0:HI]).then_inc(s["total_T_mm"], 1)
            tile_starts(0)
            for g in range(GROUPS):
                if g + EARLY < GROUPS:
                    pairs(g + EARLY)
                if g + 1 < GROUPS:
                    tile_starts(g + 1)
                find(g)
                if g % 2 == 1 and g >= 5:
                    index(g // 2 - 2)
            for q in range(GROUPS // 2 - 2, ROUNDS):
                index(q)
            pe.wait_ge(s["src_sorted_ready"], 1)
            pe.matmul(bank[7][:, 0:TILES], take_next[:, :], src_sorted[:, 1:TILES + 1], start=True, stop=False)
            pe.matmul(bank[7][:, 0:TILES], wrap_next[:, :], src_sorted[:, 2:TILES + 2], start=False, stop=True
                      ).then_inc(s["shift_mm"], 1)
            pe.matmul(bank[2][:, 0:TILES], take_prev[:, :], src_sorted[:, 1:TILES + 1], start=True, stop=False)
            pe.matmul(bank[2][:, 0:TILES], wrap_prev[:, :], src_sorted[:, 0:TILES], start=False, stop=True
                      ).then_inc(s["shift_mm"], 1)
            pe.wait_ge(s["mid_low"], 1)
            pe.wait_ge(s["wn2_lo"], C)
            for c in range(C):
                mm = product(pe, bank[3][:, :], mid_hi[:, c:c + 1].broadcast_to([P, P]),
                             mid_lo[:, c:c + 1].broadcast_to([P, P]), wn2_hi[:, c, :], wn2_lo[:, c, :], c == 0, c == C - 1)
            mm.then_inc(s["row_mm"], 1)
            pe.wait_ge(s["index_ready"], 1)

            def attr_transposes(m, i, b):
                pe.wait_ge(attr_in[b], 16 * J * (i + 1))
                need(pe, "attr_T_lo_ready", m)
                for j in range(J):
                    mm = pe.transpose(bank[4][:, P * j:P * j + P], attr[:, b, j, :], ident[:, :])
                mm.then_inc(s["attr_T_mm"], 1)

            def row_transposes(m, i, b, chunks):
                pe.wait_ge(xd_in[b], 16 * J * (i + 1))
                for c in chunks:
                    if c >= 2 or not (isinstance(m, int) and m == 0):
                        pe.wait_ge(s["xd_T_ready"], C * m + c - 1)
                    for j in range(J):
                        mm = pe.transpose(bank[5 + c % 2][:, P * j:P * j + P], xd[:, b, j, P * c:P * c + P],
                                          ident[:, :])
                    mm.then_inc(s["xd_T_mm"], 1)

            def mask(m):
                need(pe, "scan_done", C * m)
                for j in range(J):
                    mm = pe.matmul(bank[7][:, P * j:P * j + P],
                                   same_as_before[:, bass.ds(m * J + j, 1)].broadcast_to([P, P]),
                                   ident_bf[:, :], start=True, stop=True)
                mm.then_inc(s["mask_mm"], 1)

            def layer1(m):
                pe.wait_ge(s["attr_T_hi_ready"], m + 1)
                pe.wait_ge(s["attr_T_lo_ready"], m + 1)
                if isinstance(m, int) and m == 0:
                    pe.wait_ge(s["we_lo"], 1)
                for c in range(C):
                    need(pe, "msg_ready", C * (m - 1) + c + 1)
                    w = slice(P * c, P * c + P)
                    product(pe, bank[c][:, :], we1_hi[:, w], we1_lo[:, w], attr_T_hi[:, :], attr_T_lo[:, :],
                            True, True).then_inc(s["h_mm"], 1)

            attr_transposes(0, 0, 0)
            pe.wait_ge(s["row_ready"], 1)
            layer1(0)
            row_transposes(0, 0, 0, range(C))
            mask(0)

            def step(m, i, b):
                if isinstance(m, int) and m == 0:
                    pe.wait_ge(s["we_lo"], 1 + C)
                for c in range(C):
                    if c == 1 and not is_last(m):
                        attr_transposes(m + 1, i if b == 0 else i + 1, 1 - b)
                    need(pe, "z_ready", C * (m - 1) + c + 1)
                    for k in range(C):
                        if c == 0:
                            pe.wait_ge(s["h_silu"], C * m + k + 1)
                            pe.wait_ge(s["h_lo_ready"], C * m + k + 1)
                        w = slice(P * c, P * c + P)
                        mm = product(pe, bank[c][:, :], we2_hi[:, k, w], we2_lo[:, k, w], h_hi[:, k, :],
                                     h_lo[:, k, :], k == 0, k == C - 1)
                    mm.then_inc(s["ef_mm"], 1)
                if not is_last(m):
                    layer1(m + 1)
                if isinstance(m, int) and m == 0:
                    pe.wait_ge(s["wn1_lo"], C)
                for c in range(C):
                    if c == C - 1 and not is_last(m):
                        row_transposes(m + 1, i if b == 0 else i + 1, 1 - b, range(0, 2))
                    if is_last(m):
                        pe.wait_ge(s["msg_ready"], C * m + c + 1)
                    else:
                        pe.wait_ge(s["h_silu"], C * (m + 1) + c + 1)
                    for k in range(C):
                        if c == 0:
                            pe.wait_ge(s["agg_hi_ready"], C * m + k + 1)
                            pe.wait_ge(s["agg_lo_ready"], C * m + k + 1)
                        w = slice(P * c, P * c + P)
                        mm = product(pe, bank[c][:, :], wn1_hi[:, k, w], wn1_lo[:, k, w], agg_hi[:, k, :],
                                     agg_lo[:, k, :], k == 0, k == C - 1)
                    mm.then_inc(s["u_mm"], 1)
                if not is_last(m):
                    row_transposes(m + 1, i if b == 0 else i + 1, 1 - b, range(2, C))
                    mask(m + 1)
                for j in range(J):
                    pe.wait_ge(s["u_silu"], C * m + j + 1)
                    for k in range(C):
                        if j == 0:
                            pe.wait_ge(s["u_silu"], C * m + k + 1)
                            pe.wait_ge(s["u_lo_ready"], C * m + k + 1)
                        w = slice(P * j, P * j + P)
                        mm = product(pe, bank[j][:, :], u_hi[:, k, w], u_lo[:, k, w], wn2_hi[:, k, :],
                                     wn2_lo[:, k, :], k == 0, k == C - 1)
                    mm.then_inc(s["y_mm"], 1)

            steps(pe, step)

        @block.vector
        def _(dve):
            dve.wait_ge(s["numbers_ready"], 2)
            dve.wait_ge(s["src_in"], 16)
            nc.vector.tensor_scalar(node_part[:, 0, :], edge_int[:, 2, :], 7, None, ALU.logical_shift_right
                                    ).then_inc(s["parts"], 1)
            nc.vector.tensor_scalar(node_part[:, 1, :], edge_int[:, 2, :], P - 1, None, ALU.bitwise_and
                                    ).then_inc(s["parts"], 1)
            dve.wait_ge(s["parts"], 2)

            def one_hot(target, width, number, n):
                return nc.vector.tensor_tensor(target, iota_int[0:RP, 0:width].unsqueeze(1).broadcast_to([RP, n, width]),
                                               number.unsqueeze(2).broadcast_to([RP, n, width]), ALU.is_equal)

            for q in range(ROUNDS):
                t = slice(8 * q, 8 * q + 8)
                one_hot(is_hi[:, t, :], HI, node_part[:, 0, t], 8).then_inc(s["one_hots"], 1)
                one_hot(is_lo[:, t, :], P, node_part[:, 1, t], 8).then_inc(s["one_hots"], 1)
            for g in range(POOL_COPIES, GROUPS):
                t = slice(4 * g, 4 * g + 4)
                dve.wait_ge(s["hi_T_ready"], g + 1)
                nc.vector.tensor_copy(is_hi_T_bf[:, t, :], is_hi_T[:, t, 0:RP].bitcast(F32)
                                      ).then_inc(s["hi_T_bf_dve"], 1)
            dve.wait_ge(s["pool_const"], POOL_CONSTS)
            dve.wait_ge(s["counted_mm"], 3)
            nc.vector.tensor_tensor_scan(up_to[:, :], ones[:, :], counted(GROUPS), zero_col[:, 0:1], ALU.mult, ALU.add
                                         ).then_inc(s["up_to_ready"], 1)
            nc.vector.tensor_copy(total[:, :], counted(GROUPS)).then_inc(s["total_copied"], 1)
            dve.wait_ge(s["below_mm"], 1)
            nc.vector.tensor_scalar(below[:, :], bank[4][0:HI, 0:1], -float(CENTRE), None, ALU.add
                                    ).then_inc(s["start_chain"], 1)
            dve.wait_ge(s["start_chain"], 1)
            dve.wait_ge(s["total_copied"], 1)
            nc.vector.scalar_tensor_tensor(out=start[:, :], in0=up_to[:, :], scalar=below[:, 0:1], in1=total[:, :],
                                           op0=ALU.add, op1=ALU.subtract).then_inc(s["start_chain"], 1)
            dve.wait_ge(s["start_chain"], 2)
            nc.vector.tensor_copy(group_start[:, 0, :], start[:, :]).then_inc(s["start_ready"], 1)
            for n, b in enumerate((0, 1, 3)):
                first, last = 4 * n + 1, min(4 * n + 4, GROUPS - 1)
                k = last - first + 1
                nc.vector.tensor_tensor(group_start[:, first:last + 1, :],
                                        bank[b][0:HI, 0:P * k].rearrange("p (k n) -> p k n", k=k),
                                        start[:, :].unsqueeze(1).broadcast_to([HI, k, P]), ALU.add
                                        ).then_inc(s["start_ready"], 1)
            dve.wait_ge(s["dst_in"], 16)
            nc.vector.tensor_scalar(low_int[:, :, :], edge_int[:, :, :], LOW - 1, None, ALU.bitwise_and
                                    ).then_inc(s["vals_ready"], 1)
            nc.vector.tensor_scalar(high_int[:, :, :], edge_int[:, :, :], 12, None, ALU.logical_shift_right
                                    ).then_inc(s["vals_ready"], 1)
            dve.wait_ge(s["total_T_ready"], 1)
            nc.vector.tensor_scalar(touched[:, :], total_T[:, :], 1.0, float(FAR), ALU.min, ALU.mult
                                    ).then_inc(s["base_index_ready"], 1)
            dve.wait_ge(s["vals_ready"], 2)
            nc.vector.tensor_scalar(vals[:, :, 0:3].rearrange("p t v -> p v t"), low_int[:, :, :],
                                    -float(LOW // 2), None, ALU.add).then_inc(s["vals_ready"], 1)
            nc.vector.scalar_tensor_tensor(out=high_two[:, :], in0=high_int[:, 1, :], scalar=4.0,
                                           in1=high_int[:, 0, :], op0=ALU.mult, op1=ALU.add
                                           ).then_inc(s["vals_ready"], 1)
            dve.wait_ge(s["base_index_ready"], 1)
            nc.vector.tensor_tensor(base_index[:, 0:HI], node_int[:, 0:HI], touched[:, :], ALU.add
                                    ).then_inc(s["base_index_ready"], 1)
            dve.wait_ge(s["vals_ready"], 4)
            nc.vector.scalar_tensor_tensor(out=vals[:, :, 3], in0=high_int[:, 2, :], scalar=16.0,
                                           in1=high_two[:, :], op0=ALU.mult, op1=ALU.add
                                           ).then_inc(s["vals_ready"], 1)
            dve.wait_ge(s["mid_split"], 1)
            nc.vector.tensor_tensor(mid_lo[:, :], mid[:, :], mid_hi[:, :].bitcast(F32),
                                    ALU.subtract).then_inc(s["mid_low"], 1)
            for q in range(ROUNDS):
                r = slice(8 * q, 8 * q + 8)
                for t in range(8 * q, 8 * q + 8):
                    dve.wait_ge(s["find_mm"], t // 4 + 1)
                    need(dve, "found_done", t - 3)
                    nc.vector.scalar_tensor_tensor(
                        out=scrap[:, t % 4, :], in0=bank[(4, 6)[t // 4 % 2]][0:RP, P * (t % 4):P * (t % 4) + P],
                        scalar=1.0, in1=is_lo[:, t, :], op0=ALU.mult, op1=ALU.mult,
                        accum_out=found[:, t:t + 1]).then_inc(s["found_done"], 1)
                dve.wait_ge(s["found_done"], 8 * q + 8)
                nc.vector.tensor_scalar(pos_int[:, 0, r], found[:, r], float(CENTRE), None, ALU.add
                                        ).then_inc(s["rank_chain"], 1)
                dve.wait_ge(s["rank_chain"], 3 * q + 1)
                nc.vector.tensor_scalar(pos_int[:, 1, r], pos_int[:, 0, r], 7, None, ALU.logical_shift_right
                                        ).then_inc(s["rank_chain"], 1)
                nc.vector.tensor_scalar(pos_int[:, 2, r], pos_int[:, 0, r], P - 1, None, ALU.bitwise_and
                                        ).then_inc(s["rank_chain"], 1)
                dve.wait_ge(s["rank_chain"], 3 * q + 3)
                need(dve, "spread_ready", q - 1)
                one_hot(is_tile[:, q % 2, :, :], TILES, pos_int[:, 1, r], 8).then_inc(s["is_tile_ready"], 1)
                need(dve, "index_mm", q - 1)
                one_hot(is_slot[:, q % 2, :, :], P, pos_int[:, 2, r], 8).then_inc(s["is_slot_ready"], 1)
            dve.wait_ge(s["index_mm"], ROUNDS)
            nc.vector.tensor_scalar(sorted_low[:, :, :].rearrange("p v a -> p (v a)"), bank[5][:, 0:3 * TILES],
                                    float(LOW // 2), None, ALU.add).then_inc(s["index_chain"], 1)
            nc.vector.tensor_copy(sorted_high[:, :], bank[5][:, 3 * TILES:4 * TILES]).then_inc(s["index_chain"], 1)
            dve.wait_ge(s["index_chain"], 2)
            for v in range(3):
                nc.vector.tensor_scalar(sorted_top[:, v, :], sorted_high[:, :], 3 << (2 * v), 12 - 2 * v,
                                        ALU.bitwise_and, ALU.logical_shift_left).then_inc(s["index_chain"], 1)
            dve.wait_ge(s["index_chain"], 5)
            nc.vector.tensor_tensor(src_sorted[:, 1:TILES + 1], sorted_low[:, 2, :], sorted_top[:, 2, :], ALU.add
                                    ).then_inc(s["index_chain"], 1)
            nc.vector.tensor_tensor(gather_index[:, 0:2, :], sorted_low[:, 0:2, :], sorted_top[:, 0:2, :], ALU.add
                                    ).then_inc(s["edges_ready"], 1)
            dve.wait_ge(s["index_chain"], 6)
            nc.vector.tensor_tensor(src_sorted[:, TILES:TILES + 1], src_sorted[:, TILES:TILES + 1],
                                    pad_far[:, :], ALU.add).then_inc(s["src_sorted_ready"], 1)
            dve.wait_ge(s["src_sorted_ready"], 1)
            nc.vector.tensor_scalar(gather_index[:, 2, :], src_sorted[:, 1:TILES + 1], float(N - 1), None,
                                    ALU.min).then_inc(s["index_chain"], 1)
            dve.wait_ge(s["shift_mm"], 2)
            nc.vector.tensor_tensor(same_as_next[:, :], bank[7][:, 0:TILES], src_sorted[:, 1:TILES + 1],
                                    ALU.is_equal).then_inc(s["index_chain"], 1)
            nc.vector.tensor_tensor(same_as_before[:, :], bank[2][:, 0:TILES], src_sorted[:, 1:TILES + 1],
                                    ALU.is_equal).then_inc(s["index_chain"], 1)
            dve.wait_ge(s["index_chain"], 9)
            nc.vector.scalar_tensor_tensor(out=store_index[:, :], in0=same_as_next[:, :], scalar=float(FAR),
                                           in1=src_sorted[:, 1:TILES + 1], op0=ALU.mult, op1=ALU.add
                                           ).then_inc(s["index_ready"], 1)
            for name, hi, lo, raw, n, done in (
                    [("we_hi", we1_hi[:, :], we1_lo[:, :], we1_raw[:, :], 1, "we_lo")]
                    + [("we_hi", we2_hi[:, c, :], we2_lo[:, c, :], we2_raw[:, c, :], c + 2, "we_lo") for c in range(C)]
                    + [("wn1_hi", wn1_hi[:, c, :], wn1_lo[:, c, :], wn1_raw[:, c, :], c + 1, "wn1_lo")
                       for c in range(C)]):
                dve.wait_ge(s[name], n)
                nc.vector.tensor_tensor(lo, raw, hi.bitcast(F32), ALU.subtract).then_inc(s[done], 1)

            dve.wait_ge(s["row_mm"], 1)
            dve.wait_ge(s["bn2_halved"], 1)
            nc.vector.scalar_tensor_tensor(out=row_half[:, :], in0=bank[3][:, :], scalar=0.5,
                                           in1=bn2_half[:, :], op0=ALU.mult, op1=ALU.add
                                           ).then_inc(s["row_ready"], 1)
            def low(target, whole, high, name):
                nc.vector.tensor_tensor(target, whole, high.bitcast(F32), ALU.subtract).then_inc(s[name], 1)

            def split_attr(m):
                dve.wait_ge(s["attr_T_hi_ready"], m + 1)
                low(attr_T_lo[:, :], bank[4][:, :], attr_T_hi[:, :], "attr_T_lo_ready")

            def hidden_low(m, bias=False):
                for c in range(C):
                    dve.wait_ge(s["h_silu"], C * m + c + 1)
                    low(h_lo[:, c, :], silu[:, c % 2, :], h_hi[:, c, :], "h_lo_ready")
                    if bias:
                        bias_rows(m - 1, c)

            def agg_low(m, c):
                dve.wait_ge(s["agg_hi_ready"], C * m + c + 1)
                low(agg_lo[:, c, :], agg_T[:, c % 2, :], agg_hi[:, c, :], "agg_lo_ready")

            def base_add(m, i, b, half, k, name):
                n = base_rows(m, half, k)
                if k == 0:
                    dve.wait_ge(base_in[b][half], 16 * (i + 1) + (16 if base_rows(m, half, J - 1) < P and n == P
                                                                  and isinstance(m, int) else 0))
                if n:
                    t = base[0:n, b, half, k, :]
                    nc.vector.tensor_tensor(t, t, row_half[0:n, :], ALU.add).then_inc(s[name], 1)

            def moments(m, which, k, n, rows, stat, aggr, eps, last):
                nc.vector.bn_stats(stats[0:n, which, k, :], rows).then_inc(s[stat], 1)
                need(dve, stat, J * m + k + 1, True)
                nc.vector.bn_aggr(mean_var[0:n, which, k, :], stats[0:n, which, k, :]).then_inc(s[aggr], 1)
                if last:
                    need(dve, "rstd_ready", moments_made(which, m - 1))
                    dve.wait_ge(s[aggr], J * m + k + 1)
                    nc.vector.tensor_scalar(var_eps[:, which, :], mean_var[:, which, :, 1], eps, None, ALU.add
                                            ).then_inc(s["var_ready"], 1)

            def base_moments(m, b, half, k, added, which, stat, aggr):
                n = base_rows(m, half, k)
                if n:
                    dve.wait_ge(s[added], J * m + k + 1)
                    moments(m, which, k, n, base[0:n, b, half, k, :], stat, aggr, EPS / 4,
                            k == J - 1 or not base_rows(m, half, k + 1))

            def shift_of(which, m):
                dve.wait_ge(s["rstd_ready"], moments_made(which, m))
                mean = mean_var[:, 0:1, :, 0] if which == HALF_A else mean_var[:, 1:3, :, 0]
                nc.vector.scalar_tensor_tensor(out=together(shift, which), in0=mean, scalar=-1.0,
                                               in1=together(rstd, which), op0=ALU.mult, op1=ALU.mult
                                               ).then_inc(s["shift_ready"], 1)

            def bias_rows(m, j):
                dve.wait_ge(s["xs_in"], 16 * J * (m + 1))
                nc.vector.tensor_tensor(xs[:, j, :], xs[:, j, :], bn2_half[:, :], ALU.add
                                        ).then_inc(s["xs_biased"], 1)

            dve.wait_ge(s["be2_in"], 16)
            split_attr(0)
            hidden_low(0)

            def step(m, i, b):
                for c in range(C):
                    dve.wait_ge(s["ef_mm"], C * m + c + 1)
                    dve.wait_ge(s["xd_T_ready"], C * m + c + 1)
                    nc.vector.scalar_tensor_tensor(out=msg_T[:, c % 2, :], in0=bank[c][:, :],
                                                   scalar=be2_col[:, c:c + 1], in1=xd_T[:, c, :],
                                                   op0=ALU.add, op1=ALU.mult).then_inc(s["msg_ready"], 1)
                    if c == 0:
                        dve.wait_ge(s["mask_mm"], m + 1)
                        need(dve, "u_mm", C * m)
                        need(dve, "carried", C * m)
                    else:
                        agg_low(m, c - 1)
                    if c == 2 and not is_last(m):
                        split_attr(m + 1)
                    dve.wait_ge(s["msg_ready"], C * m + c + 1)
                    nc.vector.tensor_tensor_scan(agg_T[:, c % 2, :], bank[7][:, :], msg_T[:, c % 2, :],
                                                 carry[:, c:c + 1], ALU.mult, ALU.add
                                                 ).then_inc(s["scan_done"], 1)
                    if c == 0 and not (isinstance(m, int) and m == 0):
                        shift_of(HALF_B, m - 1)
                    dve.wait_ge(s["scan_done"], C * m + c + 1)
                    nc.vector.tensor_copy(carry[:, c:c + 1], agg_T[:, c % 2, M - 1:M]).then_inc(s["carried"], 1)
                agg_low(m, C - 1)
                if is_last(m):
                    for j in range(J):
                        bias_rows(m, j)
                else:
                    hidden_low(m + 1, True)
                for c in range(C):
                    base_moments(m, b, 0, c, "base_added_a", HALF_A, "dve_stats_a", "aggr_a")
                    base_add(m, i, b, 1, c, "base_added_b")
                    dve.wait_ge(s["u_silu"], C * m + c + 1)
                    low(u_lo[:, c, :], silu[:, c % 2, :], u_hi[:, c, :], "u_lo_ready")
                for j in range(J):
                    base_moments(m, b, 1, j, "base_added_b", HALF_B, "dve_stats_b", "aggr_b")
                    dve.wait_ge(s["y_mm"], C * m + j + 1)
                    if j == 0:
                        dve.wait_ge(s["xs_biased"], J * (m + 1))
                        need(dve, "out_stored", 16 * J * m)
                    nc.vector.scalar_tensor_tensor(out=z[:, j, :], in0=xs[:, j, :], scalar=2.0,
                                                   in1=bank[j][:, :], op0=ALU.mult, op1=ALU.add
                                                   ).then_inc(s["z_ready"], 1)
                    dve.wait_ge(s["z_ready"], J * m + j + 1)
                    moments(m, OUT, j, P, z[:, j, :], "dve_stats_out", "aggr_out", EPS, j == J - 1)
                    if j == 0:
                        shift_of(HALF_A, m)

            steps(dve, step)
            shift_of(HALF_B, MACROS - 1)


POOL_CONSTS = 22


_INS = ["x", "src", "dst", "edge_attr_128", "L0_gnn_We1", "L0_gnn_be1", "L0_gnn_We2", "L0_gnn_be2",
        "L0_gnn_Wn1", "L0_gnn_bn1", "L0_gnn_Wn2", "L0_gnn_bn2"]


def kernel(**inputs):
    import numpy as np
    import concourse.bacc as bacc
    from concourse.bass_utils import run_bass_kernel_spmd

    nc = bacc.Bacc("TRN2", target_bir_lowering=False, num_devices=1)
    arrays, args = {}, []
    for name in _INS:
        a = np.ascontiguousarray(inputs[name])
        arrays[f"in_{name}"] = a
        args.append(nc.dram_tensor(f"in_{name}", a.shape, mybir.dt.from_np(a.dtype), kind="ExternalInput").ap())
    shape = arrays["in_x"].shape
    args.append(nc.dram_tensor("out_rows", shape, F32, kind="ExternalOutput").ap())
    gnn_kernel(nc, *args)
    r = run_bass_kernel_spmd(nc, [arrays], core_ids=[0])
    return r.results[0]["out_rows"]
```

```python
from contextlib import ExitStack

import concourse.bass as bass
from concourse import mybir

F32 = mybir.dt.float32
F32R = mybir.dt.float32r
BF16 = mybir.dt.bfloat16
F16 = mybir.dt.float16
I32 = mybir.dt.int32
ALU = mybir.AluOpType
ACT = mybir.ActivationFunctionType

P = 128
EPS = 1e-5
FAR = 16384


def gnn_kernel(nc, x, src, dst, edge_attr, we1, be1, we2, be2, wn1, bn1, wn2, bn2, out):
    N, H = x.shape
    E, R = edge_attr.shape
    assert R == P and H % P == 0 and H <= 512 and N < FAR
    C = H // P
    J = 4
    M = J * P
    MACROS = -(-E // M)
    TILES = MACROS * J
    PAIRS = MACROS // 2
    assert MACROS % 2 == 0 and PAIRS >= 3 and C == J
    assert E % 2 == 0 and E > (TILES - 1) * P
    NT = -(-N // P)
    assert 2 * J * (MACROS - 1) < NT <= 2 * J * MACROS and NT <= TILES * 2
    RT = 40
    RP = E // RT
    assert RP * RT == E and RP <= P and RT % 8 == 0
    GROUPS = RT // 4
    ROUNDS = RT // 8
    HI = 80
    assert NT <= HI
    CENTRE = E // 2
    assert CENTRE < 4096
    VALS = 4
    LOW = 4096
    assert N <= 4 * LOW and E <= 4 * LOW

    with ExitStack() as ctx:
        def sb(name, shape, dt=F32, stack=ctx):
            return stack.enter_context(nc.sbuf_tensor(name, shape, dt))

        def sem(name):
            return ctx.enter_context(nc.semaphore(name))

        bank = [ctx.enter_context(nc.psum_tensor(f"bank{n}", [P, 512], F32)) for n in range(8)]

        we1_hi, we1_lo = sb("we1_hi", [P, H], F32R), sb("we1_lo", [P, H], F32R)
        we2_hi, we2_lo = sb("we2_hi", [P, C, H], F32R), sb("we2_lo", [P, C, H], F32R)
        wn1_hi, wn1_lo = sb("wn1_hi", [P, C, H], F32R), sb("wn1_lo", [P, C, H], F32R)
        wn2_hi, wn2_lo = sb("wn2_hi", [P, C, H], F32R), sb("wn2_lo", [P, C, H], F32R)
        be1_col, be2_col, bn1_col = sb("be1_col", [P, C]), sb("be2_col", [P, C]), sb("bn1_col", [P, C])
        bn2_half = sb("bn2_half", [P, H])
        row_half = sb("row_half", [P, H])
        ident, ident_bf = sb("ident", [P, P]), sb("ident_bf", [P, P], BF16)
        minus_half = sb("minus_half", [P, 2 * J])
        gather_index = sb("gather_index", [P, 3, TILES], I32)
        store_index = sb("store_index", [P, TILES], I32)
        base_index = sb("base_index", [P, 2 * TILES], I32)
        same_as_before = sb("same_as_before", [P, TILES], BF16)
        carry = sb("carry", [P, C])
        z = sb("z", [P, J, H])

        with ExitStack() as loading:
            we1_raw = sb("we1_raw", [P, H], stack=loading)
            we2_raw, wn1_raw, wn2_raw = (sb(f"{w}_raw", [P, C, H], stack=loading) for w in ("we2", "wn1", "wn2"))
            counts = sb("counts", [HI, GROUPS, P], F16, loading)
            scrap = sb("scrap", [RP, 4, P], stack=loading)
        base = sb("base", [P, 2, 2, J, H])

        with ExitStack() as early:
            def eb(name, shape, dt=F32):
                return sb(name, shape, dt, early)

            is_hi_T = eb("is_hi_T", [HI, RT, P], F32R)
            is_hi_T_bf = eb("is_hi_T_bf", [HI, RT, RP], BF16)
            edge_int = eb("edge_int", [RP, 3, RT], I32)
            node_part = eb("node_part", [RP, 2, RT], I32)
            low_int, high_int = eb("low_int", [RP, 3, RT], I32), eb("high_int", [RP, 3, RT], I32)
            high_two = eb("high_two", [RP, RT])
            vals = eb("vals", [RP, RT, VALS], F16)
            iota_int = eb("iota_int", [P, P], I32)
            node_int = eb("node_int", [P, 2 * TILES], I32)
            later = eb("later", [P, P])
            take_next, wrap_next = eb("take_next", [P, P]), eb("wrap_next", [P, P])
            take_prev, wrap_prev = eb("take_prev", [P, P]), eb("wrap_prev", [P, P])
            pad_far = eb("pad_far", [P, 1])
            is_lo = eb("is_lo", [RP, RT, P], BF16)
            is_hi = eb("is_hi", [RP, RT, HI], BF16)
            up_to = eb("up_to", [HI, P])
            below = eb("below", [HI, 1])
            start = eb("start", [HI, P])
            ones, zero_col = eb("ones", [HI, P]), eb("zero_col", [HI, 1])
            silu_of_zero = eb("silu_of_zero", [HI, 1])
            ident_16 = eb("ident_16", [HI, HI], F16)
            total = eb("total", [HI, P])
            group_start = eb("group_start", [HI, GROUPS, P], F32R)
            start_of = eb("start_of", [HI, RT, P], F32R)
            ident_r = eb("ident_r", [HI, HI], F32R)
            total_T = eb("total_T", [P, HI])
            touched = eb("touched", [P, HI])
            found = eb("found", [RP, RT])
            same_hi = eb("same_hi", [RP, RT, RP], BF16)
            pos_int = eb("pos_int", [RP, 3, RT], I32)
            is_slot = eb("is_slot", [RP, 3, 8, P], F16)
            is_tile = eb("is_tile", [RP, 3, 8, TILES], F16)
            spread = eb("spread", [RP, 3, 8, VALS, TILES], F16)
            sorted_low = eb("sorted_low", [P, 3, TILES], I32)
            sorted_high = eb("sorted_high", [P, TILES], I32)
            sorted_top = eb("sorted_top", [P, 3, TILES], I32)
            src_sorted = eb("src_sorted", [P, TILES + 2])
            same_as_next = eb("same_as_next", [P, TILES])
            bn2_row = eb("bn2_row", [P, H])
            mid = eb("mid", [P, C])
            mid_hi, mid_lo = eb("mid_hi", [P, C], F32R), eb("mid_lo", [P, C], F32R)

        attr = sb("attr", [P, 2, J, R])
        xd = sb("xd", [P, 2, J, H])
        xs = sb("xs", [P, J, H])
        attr_T_hi, attr_T_lo = sb("attr_T_hi", [P, M], F32R), sb("attr_T_lo", [P, M], F32R)
        h_hi, h_lo = sb("h_hi", [P, C, M], F32R), sb("h_lo", [P, C, M], F32R)
        u_hi, u_lo = sb("u_hi", [P, C, M], F32R), sb("u_lo", [P, C, M], F32R)
        agg_hi, agg_lo = sb("agg_hi", [P, C, M], F32R), sb("agg_lo", [P, C, M], F32R)
        xd_T = sb("xd_T", [P, C, M])
        msg_T = sb("msg_T", [P, 2, M])
        agg_T = sb("agg_T", [P, 2, M])
        silu = sb("silu", [P, 2, M])
        gather_now = sb("gather_now", [P, 2, 2, J], I32)
        own_now = sb("own_now", [P, 2, J], I32)
        store_now = sb("store_now", [P, 2, J], I32)
        base_now = sb("base_now", [P, 2, 2, J], I32)
        stats = sb("stats", [P, 3, J, 6])
        mean_var = sb("mean_var", [P, 3, J, 2])
        var_eps, rstd = sb("var_eps", [P, 3, J]), sb("rstd", [P, 3, J])
        shift = sb("shift", [P, 3, J])
        HALF_A, HALF_B, OUT, OUT_END = 0, 1, 2, 3
        SPLIT = J // 2

        s = {name: sem(name) for name in (
            "src_in dst_in be1_in be2_in bn1_in bn2_in we1_in we2_in wn1_in wn2_in "
            "numbers_ready pool_const consts_r_ready we_hi wn1_hi wn2_hi we_lo wn1_lo wn2_lo "
            "bn2_halved mid_split mid_low row_mm row_ready "
            "parts one_hots vals_ready counts_mm counts_ready counted_mm up_to_ready below_mm start_chain "
            "total_copied total_T_mm total_T_ready start_ready tile_start_mm tile_start_ready "
            "hi_T_mm hi_T_ready hi_T_bf_pool hi_T_bf_dve same_hi_mm same_hi_copied same_hi_ready "
            "find_mm found_done rank_chain is_tile_ready is_slot_ready spread_ready spread_end index_mm "
            "index_chain edges_ready src_sorted_ready shift_mm index_ready base_index_ready "
            "attr_T_mm attr_T_hi_ready attr_T_lo_ready h_mm h_silu h_lo_ready ef_mm msg_ready scan_done carried "
            "agg_hi_ready agg_lo_ready u_mm u_silu u_lo_ready xd_T_mm xd_T_ready mask_mm y_mm z_ready "
            "stats_a stats_b stats_out base_added_a base_added_b aggr_a aggr_b aggr_out "
            "rows_a rows_b rows_out var_ready rstd_ready shift_ready "
            "copied_gather copied_own copied_store copied_base xs_biased xs_in out_stored passed"
        ).split()}
        attr_in = [sem(f"attr_in{b}") for b in range(2)]
        xd_in = [sem(f"xd_in{b}") for b in range(2)]
        base_in = [[sem(f"base_in{b}{h}") for h in range(2)] for b in range(2)]
        base_stored = [[sem(f"base_stored{b}{h}") for h in range(2)] for b in range(2)]

        def need(eng, name, count, alone=False):
            if isinstance(count, int) and count <= 0:
                return
            eng.wait_ge(s[name] if isinstance(name, str) else name, count)
            if alone and not isinstance(count, int):
                eng.sem_inc(s["passed"], 1)

        def steps(eng, step):
            for b in range(2):
                step(b, 0, b)
            with eng.Fori(1, PAIRS - 1) as i:
                for b in range(2):
                    step(2 * i + b, i, b)
            for b in range(2):
                step(MACROS - 2 + b, PAIRS - 1, b)

        def is_last(m):
            return isinstance(m, int) and m == MACROS - 1

        EARLY = 6
        POOL_COPIES = 4
        assert GROUPS - EARLY <= 4

        def counts_bank(g):
            return bank[(4, 6)[g % 2]][0:HI, 0:P]

        def counted(g):
            at = (g - 1) % 4
            return bank[(0, 1, 3)[(g - 1) // 4]][0:HI, P * at:P * at + P]

        def spread_tiles(engine, q, first, end):
            n = end - first
            shape = [RP, n, VALS, TILES]
            return engine.tensor_tensor(
                spread[:, q % 3, first:end, :, :], is_tile[:, q % 3, first:end, :].unsqueeze(2).broadcast_to(shape),
                vals[:, 8 * q + first:8 * q + end, :].unsqueeze(3).broadcast_to(shape), ALU.mult)

        def same_hi_bank(g):
            return bank[(2, 7)[g % 2]][0:RP, 0:4 * RP].rearrange("p (k e) -> p k e", k=4)

        def width(m):
            return E - (MACROS - 1) * M if is_last(m) else M

        def edge_rows(m, j):
            return min(P, width(m) - P * j)

        def base_rows(m, half, k):
            if not isinstance(m, int):
                return P
            return max(0, min(P, N - ((2 * m + half) * J + k) * P))

        def hi_T_bank(g):
            return bank[(2, 7)[g % 2]][0:HI, 0:256].bitcast(BF16).rearrange("p (k e) -> p k e", k=4)[:, :, 0:RP]

        def moments_made(which, m):
            if is_last(m):
                return 2 * m + {HALF_B: 1, HALF_A: 2, OUT: 3, OUT_END: 4}[which]
            return 2 * m + (1 if which == HALF_A else 2)

        def variances_made(which, m):
            if is_last(m):
                return 3 * m + {HALF_B: 1, HALF_A: 2, OUT: 3, OUT_END: 4}[which]
            return 3 * m + (1 if which == HALF_A else 3)

        def group(t, which, m):
            if which == HALF_A:
                return t[:, 0:1, :]
            if not is_last(m):
                return t[:, 1:3, :]
            return {HALF_B: t[:, 1:2, :], OUT: t[:, 2:3, 0:SPLIT], OUT_END: t[:, 2:3, SPLIT:J]}[which]

        block = ctx.enter_context(nc.Block())

        @block.sync
        def _(sp):
            sp.dma_start(edge_int[:, 2, :], src.rearrange("(p t) -> p t", t=RT)).then_inc(s["src_in"], 16)
            sp.dma_start(edge_int[:, 1, :], dst.rearrange("(p t) -> p t", t=RT)).then_inc(s["dst_in"], 16)
            sp.dma_start(we1_raw[:, :], we1).then_inc(s["we1_in"], 16)
            for w, r, name in ((we2, we2_raw, "we2_in"), (wn2, wn2_raw, "wn2_in"), (wn1, wn1_raw, "wn1_in")):
                sp.dma_start(r[:, :, :], w.rearrange("(c p) n -> p c n", p=P)).then_inc(s[name], 16)
            sp.wait_ge(s["wn2_lo"], C)
            sp.wait_ge(s["we_lo"], 1 + C)
            sp.wait_ge(s["wn1_lo"], C)
            sp.wait_ge(s["xd_T_mm"], 1)

            def step(m, i, b):
                for half in range(2):
                    need(sp, base_stored[b][half], 64 * i)
                    first = (2 * m + half) * J * P
                    full = sum(base_rows(m, half, k) == P for k in range(J))
                    sp.dma_start(base[:, b, half, 0:full, :],
                                 x[bass.ds(first, full * P), :].rearrange("(k p) h -> p k h", p=P)
                                 ).then_inc(base_in[b][half], 16)
                    if full < J and base_rows(m, half, full):
                        n = base_rows(m, half, full)
                        sp.dma_start(base[0:n, b, half, full, :], x[N - n:N, :]).then_inc(base_in[b][half], 16)

            steps(sp, step)

        @block.gpsimd
        def _(pool):
            consts = [0]

            def const(ins):
                ins.then_inc(s["pool_const"], 1)
                consts[0] += 1

            nc.gpsimd.iota(iota_int[:, :], [[1, P]], base=0, channel_multiplier=0
                           ).then_inc(s["numbers_ready"], 1)
            nc.gpsimd.iota(edge_int[:, 0, :], [[1, RT]], base=0, channel_multiplier=RT
                           ).then_inc(s["numbers_ready"], 1)
            for t in (ident_bf, ident, take_next, wrap_next, take_prev, wrap_prev):
                const(nc.gpsimd.memset(t[:, :], 0.0))
            const(nc.gpsimd.memset(later[:, :], 1.0))
            const(nc.gpsimd.memset(ones[:, :], 1.0))
            const(nc.gpsimd.memset(zero_col[:, :], 0.0))
            const(nc.gpsimd.memset(pad_far[:, :], float(FAR)))
            const(nc.gpsimd.memset(minus_half[:, :], -0.5))
            const(nc.gpsimd.memset(carry[:, :], 0.0))
            const(nc.gpsimd.memset(src_sorted[:, :], -1.0))
            const(nc.gpsimd.iota(node_int[:, :], [[P, 2 * TILES]], base=0, channel_multiplier=1))
            pool.wait_ge(s["pool_const"], consts[0])
            for t, at in ((ident_bf, 0), (ident, 0), (take_next, -1), (wrap_next, P - 1), (take_prev, 1),
                          (wrap_prev, -(P - 1))):
                const(nc.gpsimd.affine_select(out=t[:, :], in_=t[:, :], compare_op=ALU.not_equal, fill=1.0,
                                              base=at, pattern=[[-1, P]], channel_multiplier=1))
            const(nc.gpsimd.affine_select(out=later[:, :], in_=later[:, :], compare_op=ALU.is_gt, fill=0.0,
                                          base=0, pattern=[[1, P]], channel_multiplier=-1))
            const(nc.gpsimd.affine_select(out=pad_far[:, :], in_=pad_far[:, :], compare_op=ALU.is_ge, fill=0.0,
                                          base=-(E - (TILES - 1) * P), pattern=[[0, 1]], channel_multiplier=1))
            assert consts[0] == POOL_CONSTS

            for g in range(POOL_COPIES):
                t = slice(4 * g, 4 * g + 4)
                pool.wait_ge(s["hi_T_ready"], g + 1)
                nc.gpsimd.tensor_copy(is_hi_T_bf[:, t, :], is_hi_T[:, t, 0:RP].bitcast(F32)
                                      ).then_inc(s["hi_T_bf_pool"], 1)
            for g in range(GROUPS):
                pool.wait_ge(s["same_hi_copied"], g + 1)
                pairs = same_hi[:, 4 * g:4 * g + 4, :]
                nc.gpsimd.affine_select(out=pairs, in_=pairs, compare_op=ALU.is_gt, fill=0.0, base=0,
                                        pattern=[[0, 4], [1, RP]], channel_multiplier=-1
                                        ).then_inc(s["same_hi_ready"], 1)
                c = g - (GROUPS - C)
                if c >= 0:
                    pool.wait_ge(s["wn2_hi"], c + 1)
                    nc.gpsimd.tensor_tensor(wn2_lo[:, c, :], wn2_raw[:, c, :], wn2_hi[:, c, :].bitcast(F32),
                                            ALU.subtract).then_inc(s["wn2_lo"], 1)
            for q in range(ROUNDS):
                pool.wait_ge(s["vals_ready"], 5)
                pool.wait_ge(s["is_tile_ready"], q + 1)
                need(pool, "index_mm", q - 2)
                spread_tiles(nc.gpsimd, q, 0, 8 if q < ROUNDS - 1 else 4).then_inc(s["spread_ready"], 1)

            pool.wait_ge(s["edges_ready"], 1)

            def gather_attr(m, i, b):
                need(pool, "attr_T_mm", m - 1, True)
                need(pool, "xd_T_mm", C * (m - 1), True)
                nc.gpsimd.tensor_copy(gather_now[:, b, :, :], gather_index[:, 0:2, bass.ds(m * J, J)]
                                      ).then_inc(s["copied_gather"], 1)
                need(pool, "copied_gather", m + 1, True)
                for j in range(J):
                    pool.indirect_dma_start(
                        out=attr[:, b, j, :], out_offset=None, in_=edge_attr,
                        in_offset=bass.IndirectOffsetOnAxis(ap=gather_now[:, b, 0, j:j + 1], axis=0),
                    ).then_inc(attr_in[b], 16)

            def gather_dst(m, i, b):
                for j in range(J):
                    pool.indirect_dma_start(
                        out=xd[:, b, j, :], out_offset=None, in_=x,
                        in_offset=bass.IndirectOffsetOnAxis(ap=gather_now[:, b, 1, j:j + 1], axis=0),
                    ).then_inc(xd_in[b], 16)

            def base_add(m, i, b):
                pool.wait_ge(s["row_ready"], 1)
                need(pool, base_in[b][0], 16 * (i + 1), True)
                for k in range(J):
                    assert base_rows(m, 0, k) == P
                    t = base[:, b, 0, k, :]
                    nc.gpsimd.tensor_tensor(t, t, row_half[:, :], ALU.add).then_inc(s["base_added_a"], 1)

            def rstd_of(which, m):
                need(pool, "var_ready", variances_made(which, m), True)
                for rows in {HALF_A: ("rows_a",), HALF_B: ("rows_b", "rows_out")}.get(which, ("rows_out",)):
                    need(pool, rows, J * m, True)
                v = group(var_eps, which, m)
                g, k = v.shape[1], v.shape[2]
                nc.gpsimd.tensor_tensor(group(rstd, which, m), v,
                                        minus_half[:, 0:g * k].rearrange("p (g k) -> p g k", g=g),
                                        ALU.pow).then_inc(s["rstd_ready"], 1)

            def store_base(m, i, b, half, rows):
                for k in range(J):
                    if is_last(m) and half == 0 and k == 2:
                        rstd_of(OUT, m)
                    n = base_rows(m, half, k)
                    if n:
                        need(pool, rows, J * m + k + 1, True)
                        pool.indirect_dma_start(
                            out=out, in_=base[0:n, b, half, k, :], in_offset=None,
                            out_offset=bass.IndirectOffsetOnAxis(ap=base_now[0:n, b, half, k:k + 1], axis=0),
                            bounds_check=N - 1, oob_is_err=False).then_inc(base_stored[b][half], 16)

            def store_sorted(m, i, b):
                need(pool, "out_stored", 16 * J * (m - 1), True)
                nc.gpsimd.tensor_copy(store_now[:, b, :], store_index[:, bass.ds(m * J, J)]
                                      ).then_inc(s["copied_store"], 1)
                need(pool, "copied_store", m + 1, True)
                for j in range(J):
                    if is_last(m) and j == 1:
                        rstd_of(OUT_END, m)
                    need(pool, "rows_out", J * m + j + 1, True)
                    n = edge_rows(m, j)
                    pool.indirect_dma_start(
                        out=out, in_=z[0:n, j, :], in_offset=None,
                        out_offset=bass.IndirectOffsetOnAxis(ap=store_now[0:n, b, j:j + 1], axis=0),
                        bounds_check=N - 1, oob_is_err=False).then_inc(s["out_stored"], 16)

            def base_indices(m, i, b):
                for half in range(2):
                    need(pool, base_stored[b][half], 16 * J * i, True)
                nc.gpsimd.tensor_copy(base_now[:, b, :, :], base_index[:, bass.ds(m * 2 * J, 2 * J)]
                                      .rearrange("p (h k) -> p h k", h=2)).then_inc(s["copied_base"], 1)
                need(pool, "copied_base", m + 1, True)

            gather_attr(0, 0, 0)
            gather_dst(0, 0, 0)
            pool.wait_ge(s["index_ready"], 1)
            gather_attr(1, 0, 1)
            gather_dst(1, 0, 1)

            def step(m, i, b):
                first, more = isinstance(m, int) and m == 0, not (isinstance(m, int) and m >= MACROS - 2)
                before = (m - 1, i if b else i - 1, 1 - b)
                if not first:
                    rstd_of(HALF_B, m - 1)
                need(pool, "z_ready", J * m, True)
                nc.gpsimd.tensor_copy(own_now[:, b, :], gather_index[:, 2, bass.ds(m * J, J)]
                                      ).then_inc(s["copied_own"], 1)
                need(pool, "copied_own", m + 1, True)
                for j in range(J):
                    pool.indirect_dma_start(
                        out=xs[:, j, :], out_offset=None, in_=x,
                        in_offset=bass.IndirectOffsetOnAxis(ap=own_now[:, b, j:j + 1], axis=0),
                    ).then_inc(s["xs_in"], 16)
                if not first:
                    base_indices(*before)
                    store_base(*before, 0, "rows_a")
                if more:
                    gather_attr(m + 2, i + 1, b)
                if not first:
                    store_sorted(*before)
                if more:
                    gather_dst(m + 2, i + 1, b)
                if is_last(m):
                    rstd_of(HALF_B, m)
                if not first:
                    store_base(*before, 1, "rows_b")
                if first:
                    base_add(m, i, b)
                if not is_last(m):
                    rstd_of(HALF_A, m)
                    base_add(m + 1, i if b == 0 else i + 1, 1 - b)

            steps(pool, step)
            last = (MACROS - 1, PAIRS - 1, 1)
            base_indices(*last)
            rstd_of(HALF_A, MACROS - 1)
            store_base(*last, 1, "rows_b")
            store_base(*last, 0, "rows_a")
            store_sorted(*last)
            need(pool, "out_stored", 16 * TILES, True)
            for b in range(2):
                for half in range(2):
                    tiles = sum(base_rows(m, half, k) > 0 for m in range(b, MACROS, 2) for k in range(J))
                    pool.wait_ge(base_stored[b][half], 16 * tiles)

        @block.scalar
        def _(act):
            act.dma_start(bn2_row[:, :], bn2.rearrange("(o h) -> o h", o=1).broadcast_to([P, H])
                          ).then_inc(s["bn2_in"], 16)
            for v, t, name in ((be1, be1_col, "be1_in"), (be2, be2_col, "be2_in"), (bn1, bn1_col, "bn1_in")):
                act.dma_start(t[:, :], v.rearrange("(c p) -> p c", p=P), allow_slow_non_contiguous=True
                              ).then_inc(s[name], 16)
            act.wait_ge(s["pool_const"], POOL_CONSTS)
            nc.scalar.activation(silu_of_zero[:, :], zero_col[:, :], ACT.Silu)
            nc.scalar.activation(ident_r[:, :], ident[0:HI, 0:HI], ACT.Copy).then_inc(s["consts_r_ready"], 1)
            nc.scalar.activation(ident_16[:, :], ident[0:HI, 0:HI], ACT.Copy).then_inc(s["consts_r_ready"], 1)
            for g in range(GROUPS):
                act.wait_ge(s["counts_mm"], g + 1)
                nc.scalar.activation(counts[:, g, :], counts_bank(g), ACT.Copy).then_inc(s["counts_ready"], 1)
                act.wait_ge(s["hi_T_mm"], g + 1)
                nc.scalar.activation(is_hi_T[:, 4 * g:4 * g + 4, 0:RP],
                                     hi_T_bank(g), ACT.Copy).then_inc(s["hi_T_ready"], 1)
            highs = ([("wn2_in", wn2_hi, wn2_raw, c, "wn2_hi") for c in range(C)]
                     + [("we1_in", we1_hi, we1_raw, None, "we_hi")]
                     + [("we2_in", we2_hi, we2_raw, c, "we_hi") for c in range(C)]
                     + [("wn1_in", wn1_hi, wn1_raw, c, "wn1_hi") for c in range(C)])

            def high(name, hi, raw, c, done):
                act.wait_ge(s[name], 16)
                hi, raw = (hi[:, :], raw[:, :]) if c is None else (hi[:, c, :], raw[:, c, :])
                nc.scalar.activation(hi, raw, ACT.Copy).then_inc(s[done], 1)

            def copy_same_hi(g):
                act.wait_ge(s["same_hi_mm"], g + 1)
                nc.scalar.activation(same_hi[:, 4 * g:4 * g + 4, :], same_hi_bank(g), ACT.Copy
                                     ).then_inc(s["same_hi_copied"], 1)

            for g in range(4):
                copy_same_hi(g)
            for g in range(GROUPS):
                act.wait_ge(s["tile_start_mm"], g + 1)
                nc.scalar.activation(start_of[:, 4 * g:4 * g + 4, :].rearrange("p k n -> p (k n)"),
                                     bank[g % 2][0:HI, :], ACT.Copy).then_inc(s["tile_start_ready"], 1)
                for ahead in ((4, 5) if g == 0 else (g + 5,)):
                    if ahead < GROUPS:
                        copy_same_hi(ahead)
                if g == 0:
                    act.wait_ge(s["total_T_mm"], 1)
                    nc.scalar.activation(total_T[:, :], bank[5][0:P, 0:HI], ACT.Copy).then_inc(s["total_T_ready"], 1)
                if g == 1:
                    act.wait_ge(s["bn1_in"], 16)
                    nc.scalar.activation(mid_hi[:, :], bn1_col[:, :], ACT.Silu)
                    nc.scalar.activation(mid[:, :], bn1_col[:, :], ACT.Silu).then_inc(s["mid_split"], 1)
                    act.wait_ge(s["bn2_in"], 16)
                    nc.scalar.activation(bn2_half[:, :], bn2_row[:, :], ACT.Copy, scale=0.5
                                         ).then_inc(s["bn2_halved"], 1)
                high(*highs[g])
            for g in range(GROUPS, len(highs)):
                high(*highs[g])
            act.wait_ge(s["index_ready"], 1)

            def split_attr(m):
                act.wait_ge(s["attr_T_mm"], m + 1)
                need(act, "h_mm", C * m)
                nc.scalar.activation(attr_T_hi[:, 0:width(m)], bank[4][:, 0:width(m)], ACT.Copy
                                     ).then_inc(s["attr_T_hi_ready"], 1)

            def hidden(m, c):
                act.wait_ge(s["h_mm"], C * m + c + 1)
                if c == 0:
                    need(act, "ef_mm", C * m)
                if c >= 2:
                    need(act, "h_lo_ready", C * m + c - 1)
                else:
                    need(act, "u_lo_ready", C * (m - 2) + c + 3)
                w = slice(0, width(m))
                nc.scalar.activation(h_hi[:, c, w], bank[c][:, w], ACT.Silu, bias=be1_col[:, c:c + 1])
                nc.scalar.activation(silu[:, c % 2, w], bank[c][:, w], ACT.Silu, bias=be1_col[:, c:c + 1]
                                     ).then_inc(s["h_silu"], 1)

            def transposed_rows(m, chunks):
                for c in chunks:
                    act.wait_ge(s["xd_T_mm"], C * m + c + 1)
                    need(act, "msg_ready", C * (m - 1) + c + 1)
                    w = slice(0, width(m))
                    nc.scalar.activation(xd_T[:, c, w], bank[5 + c % 2][:, w], ACT.Copy
                                         ).then_inc(s["xd_T_ready"], 1)

            def norm_base(m, b, half, k, which, rows):
                n = base_rows(m, half, k)
                if n:
                    if k == 0:
                        act.wait_ge(s["shift_ready"], moments_made(which, m))
                    t = base[0:n, b, half, k, :]
                    nc.scalar.activation(t, t, ACT.Identity, bias=shift[0:n, which, k:k + 1],
                                         scale=rstd[0:n, which, k:k + 1]).then_inc(s[rows], 1)

            def norm_sorted(m, j):
                if j == 0:
                    act.wait_ge(s["shift_ready"], moments_made(OUT, m))
                elif is_last(m) and j == SPLIT:
                    act.wait_ge(s["shift_ready"], moments_made(OUT_END, m))
                n = edge_rows(m, j)
                nc.scalar.activation(z[0:n, j, :], z[0:n, j, :], ACT.Identity, bias=shift[0:n, OUT, j:j + 1],
                                     scale=rstd[0:n, OUT, j:j + 1]).then_inc(s["rows_out"], 1)

            act.wait_ge(s["be1_in"], 16)
            split_attr(0)
            for c in range(C):
                hidden(0, c)
            transposed_rows(0, range(C))

            def step(m, i, b):
                first = isinstance(m, int) and m == 0
                w = slice(0, width(m))
                norms = [] if first else [(OUT, k) for k in range(J)] + [(HALF_B, k) for k in range(J)]

                def norm(n):
                    for kind, k in norms[0:n]:
                        if kind == OUT:
                            norm_sorted(m - 1, k)
                        else:
                            norm_base(m - 1, 1 - b, 1, k, HALF_B, "rows_b")
                    del norms[0:n]

                if not is_last(m):
                    split_attr(m + 1)
                for c in range(C):
                    if c == C - 1 and not is_last(m):
                        hidden(m + 1, 0)
                    act.wait_ge(s["scan_done"], C * m + c + 1)
                    if c == 0:
                        need(act, "u_mm", C * m)
                    nc.scalar.activation(agg_hi[:, c, w], agg_T[:, c % 2, w], ACT.Copy
                                         ).then_inc(s["agg_hi_ready"], 1)
                    norm((2, 3, 0, 0)[c])
                for c in range(1, C):
                    if not is_last(m):
                        hidden(m + 1, c)
                    norm(1)
                for c in range(C):
                    if c == C - 2 and not is_last(m):
                        transposed_rows(m + 1, range(0, 2))
                    act.wait_ge(s["u_mm"], C * m + c + 1)
                    if c == 0:
                        need(act, "y_mm", C * m)
                    if c >= 2:
                        need(act, "u_lo_ready", C * m + c - 1)
                    elif is_last(m):
                        need(act, "u_lo_ready", C * (m - 1) + c + 3)
                    else:
                        need(act, "h_lo_ready", C * (m + 1) + c + 3)
                    nc.scalar.activation(u_hi[:, c, w], bank[c][:, w], ACT.Silu, bias=bn1_col[:, c:c + 1])
                    nc.scalar.activation(silu[:, c % 2, w], bank[c][:, w], ACT.Silu, bias=bn1_col[:, c:c + 1]
                                         ).then_inc(s["u_silu"], 1)
                if is_last(m):
                    for k in range(J):
                        norm_base(m, b, 1, k, HALF_B, "rows_b")
                else:
                    transposed_rows(m + 1, range(2, C))
                for k in range(J):
                    norm_base(m, b, 0, k, HALF_A, "rows_a")

            steps(act, step)
            for j in range(J):
                norm_sorted(MACROS - 1, j)

        def product(pe, target, lhs_hi, lhs_lo, rhs_hi, rhs_lo, start, stop):
            pe.matmul(target, lhs_lo, rhs_hi, start=start, stop=False)
            pe.matmul(target, lhs_hi, rhs_lo, start=False, stop=False)
            return pe.matmul(target, lhs_hi, rhs_hi, start=False, stop=stop)

        def layer_chunk(pe, target, pairs, ready=None):
            for k in range(C):
                if ready:
                    pe.wait_ge(s[ready[0]], ready[2] + k + 1)
                pe.matmul(target, *pairs(k)[0], start=(k == 0), stop=False)
                pe.matmul(target, *pairs(k)[1], start=False, stop=False)
            for k in range(C):
                if ready:
                    pe.wait_ge(s[ready[1]], ready[2] + k + 1)
                mm = pe.matmul(target, *pairs(k)[2], start=False, stop=(k == C - 1))
            return mm

        @block.tensor
        def _(pe):
            def add_counts(g):
                pe.wait_ge(s["counts_ready"], g + 1)
                if g == 0:
                    pe.wait_ge(s["consts_r_ready"], 2)
                for n, b in enumerate((0, 1, 3)):
                    first, last = max(g + 1, 4 * n + 1), min(4 * n + 4, GROUPS)
                    if first <= last:
                        k = last - first + 1
                        at = (first - 1) % 4
                        mm = pe.matmul(bank[b][0:HI, P * at:P * (at + k)].rearrange("p (k n) -> p k n", k=k),
                                       ident_16[:, :], counts[:, g, :].unsqueeze(1).broadcast_to([HI, k, P]),
                                       start=(g == 0), stop=(g + 1 == last))
                if g in (3, 7, GROUPS - 1):
                    mm.then_inc(s["counted_mm"], 1)

            for g in range(GROUPS):
                pe.wait_ge(s["one_hots"], 2 * (g // 2 + 1))
                need(pe, "counts_ready", g - 1)
                for t in range(4 * g, 4 * g + 4):
                    mm = pe.matmul(counts_bank(g), is_hi[:, t, :], is_lo[:, t, :], start=(t % 4 == 0),
                                   stop=(t % 4 == 3))
                mm.then_inc(s["counts_mm"], 1)
                need(pe, "hi_T_ready", g - 1)
                if g == 0:
                    pe.wait_ge(s["pool_const"], POOL_CONSTS)
                for k in range(4):
                    mm = pe.transpose(hi_T_bank(g)[:, k, :], is_hi[:, 4 * g + k, :], ident_bf[0:RP, 0:RP])
                mm.then_inc(s["hi_T_mm"], 1)
                if g:
                    add_counts(g - 1)
            add_counts(GROUPS - 1)

            def pairs(g):
                pe.wait_ge(s["hi_T_ready"], GROUPS)
                if g < POOL_COPIES:
                    pe.wait_ge(s["hi_T_bf_pool"], g + 1)
                else:
                    pe.wait_ge(s["hi_T_bf_dve"], g + 1 - POOL_COPIES)
                need(pe, "same_hi_copied", g - 1)
                for k in range(4):
                    t = 4 * g + k
                    mm = pe.matmul(same_hi_bank(g)[:, k, :], is_hi_T_bf[:, t, :], is_hi_T_bf[:, t, :], start=True,
                                   stop=True)
                mm.then_inc(s["same_hi_mm"], 1)

            pairs(0)
            pe.wait_ge(s["up_to_ready"], 1)
            pe.matmul(bank[4][0:HI, 0:1], later[0:HI, 0:HI], up_to[:, P - 1:P], start=True, stop=True
                      ).then_inc(s["below_mm"], 1)

            def tile_starts(g):
                need(pe, "tile_start_ready", g - 1)
                pe.wait_ge(s["start_ready"], max((g + 3) // 4 + 1, g % 2 + 2))
                places = bank[g % 2][0:HI, :].rearrange("p (k n) -> p k n", k=4)
                pe.matmul(places, ident_r[:, :], group_start[:, g, :].unsqueeze(1).broadcast_to([HI, 4, P]),
                          start=True, stop=False)
                for k in range(3):
                    mm = pe.matmul(places[:, k + 1:4, :], is_hi[:, 4 * g + k, :],
                                   is_lo[:, 4 * g + k, :].unsqueeze(1).broadcast_to([RP, 3 - k, P]),
                                   start=False, stop=(k == 2))
                mm.then_inc(s["tile_start_mm"], 1)

            def find(g):
                pe.wait_ge(s["tile_start_ready"], g + 1)
                pe.wait_ge(s["same_hi_ready"], g + 1)
                need(pe, "found_done", 4 * (g - 1))
                for k in range(4):
                    t = 4 * g + k
                    places = bank[(4, 6)[g % 2]][0:RP, P * k:P * k + P]
                    pe.matmul(places, is_hi_T[:, t, 0:RP], start_of[:, t, :], start=True, stop=False)
                    mm = pe.matmul(places, same_hi[:, t, :], is_lo[:, t, :], start=False, stop=True)
                mm.then_inc(s["find_mm"], 1)

            def index(q):
                pe.wait_ge(s["spread_ready"], q + 1)
                pe.wait_ge(s["is_slot_ready"], q + 1)
                if q == ROUNDS - 1:
                    pe.wait_ge(s["spread_end"], 1)
                if q == 0:
                    pe.wait_ge(s["total_T_ready"], 1)
                for k in range(8):
                    mm = pe.matmul(bank[5][:, 0:VALS * TILES], is_slot[:, q % 3, k, :],
                                   spread[:, q % 3, k, :, :].rearrange("p v a -> p (v a)"),
                                   start=(q == 0 and k == 0), stop=(q == ROUNDS - 1 and k == 7))
                mm.then_inc(s["index_mm"], 1)

            for g in range(1, EARLY):
                pairs(g)
            pe.wait_ge(s["total_copied"], 1)
            pe.transpose(bank[5][0:P, 0:HI], total[:, :], ident[0:HI, 0:HI]).then_inc(s["total_T_mm"], 1)
            tile_starts(0)
            for g in range(GROUPS):
                if g + 1 < GROUPS:
                    tile_starts(g + 1)
                find(g)
                if g + EARLY < GROUPS:
                    pairs(g + EARLY)
                if g % 2 == 1 and g >= 7:
                    index(g // 2 - 3)
            def shared_row(c):
                pe.wait_ge(s["mid_low"], 1)
                pe.wait_ge(s["wn2_lo"], c + 1)
                return product(pe, bank[3][:, :], mid_hi[:, c:c + 1].broadcast_to([P, P]),
                               mid_lo[:, c:c + 1].broadcast_to([P, P]), wn2_hi[:, c, :], wn2_lo[:, c, :], c == 0,
                               c == C - 1)

            for q in range(GROUPS // 2 - 3, ROUNDS - 2):
                index(q)
            shared_row(0)
            index(ROUNDS - 2)
            shared_row(1)
            index(ROUNDS - 1)
            pe.wait_ge(s["src_sorted_ready"], 1)
            pe.matmul(bank[7][:, 0:TILES], take_next[:, :], src_sorted[:, 1:TILES + 1], start=True, stop=False)
            pe.matmul(bank[7][:, 0:TILES], wrap_next[:, :], src_sorted[:, 2:TILES + 2], start=False, stop=True
                      ).then_inc(s["shift_mm"], 1)
            pe.matmul(bank[2][:, 0:TILES], take_prev[:, :], src_sorted[:, 1:TILES + 1], start=True, stop=False)
            pe.matmul(bank[2][:, 0:TILES], wrap_prev[:, :], src_sorted[:, 0:TILES], start=False, stop=True
                      ).then_inc(s["shift_mm"], 1)
            for c in range(2, C):
                mm = shared_row(c)
            mm.then_inc(s["row_mm"], 1)
            pe.wait_ge(s["index_ready"], 1)

            def attr_transposes(m, i, b):
                pe.wait_ge(attr_in[b], 16 * J * (i + 1))
                need(pe, "attr_T_lo_ready", m)
                for j in range(J):
                    mm = pe.transpose(bank[4][:, P * j:P * j + P], attr[:, b, j, :], ident[:, :])
                mm.then_inc(s["attr_T_mm"], 1)

            def row_transposes(m, i, b, chunks):
                pe.wait_ge(xd_in[b], 16 * J * (i + 1))
                for c in chunks:
                    if c >= 2 or not (isinstance(m, int) and m == 0):
                        pe.wait_ge(s["xd_T_ready"], C * m + c - 1)
                    for j in range(J):
                        mm = pe.transpose(bank[5 + c % 2][:, P * j:P * j + P], xd[:, b, j, P * c:P * c + P],
                                          ident[:, :])
                    mm.then_inc(s["xd_T_mm"], 1)

            def mask(m):
                need(pe, "scan_done", C * m)
                for j in range(J):
                    mm = pe.matmul(bank[7][:, P * j:P * j + P],
                                   same_as_before[:, bass.ds(m * J + j, 1)].broadcast_to([P, P]),
                                   ident_bf[:, :], start=True, stop=True)
                mm.then_inc(s["mask_mm"], 1)

            def layer1(m):
                pe.wait_ge(s["attr_T_hi_ready"], m + 1)
                if isinstance(m, int) and m == 0:
                    pe.wait_ge(s["we_lo"], 1)
                for c in range(C):
                    need(pe, "msg_ready", C * (m - 1) + c + 1)
                    w, e = slice(P * c, P * c + P), slice(0, width(m))
                    pe.matmul(bank[c][:, e], we1_lo[:, w], attr_T_hi[:, e], start=True, stop=False)
                    pe.matmul(bank[c][:, e], we1_hi[:, w], attr_T_hi[:, e], start=False, stop=False)
                    if c == 0:
                        pe.wait_ge(s["attr_T_lo_ready"], m + 1)
                    pe.matmul(bank[c][:, e], we1_hi[:, w], attr_T_lo[:, e], start=False, stop=True
                              ).then_inc(s["h_mm"], 1)

            attr_transposes(0, 0, 0)
            pe.wait_ge(s["row_ready"], 1)
            layer1(0)
            row_transposes(0, 0, 0, range(C))
            mask(0)

            def step(m, i, b):
                e = slice(0, width(m))
                if isinstance(m, int) and m == 0:
                    pe.wait_ge(s["we_lo"], 1 + C)
                for c in range(C):
                    if c == 0 and not is_last(m):
                        attr_transposes(m + 1, i if b == 0 else i + 1, 1 - b)
                    need(pe, "z_ready", C * (m - 1) + c + 1)
                    w = slice(P * c, P * c + P)
                    layer_chunk(pe, bank[c][:, e],
                                lambda k: ((we2_lo[:, k, w], h_hi[:, k, e]), (we2_hi[:, k, w], h_hi[:, k, e]),
                                           (we2_hi[:, k, w], h_lo[:, k, e])),
                                ("h_silu", "h_lo_ready", C * m) if c == 0 else None).then_inc(s["ef_mm"], 1)
                if not is_last(m):
                    layer1(m + 1)
                if isinstance(m, int) and m == 0:
                    pe.wait_ge(s["wn1_lo"], C)
                for c in range(C):
                    if c == C - 1 and not is_last(m):
                        row_transposes(m + 1, i if b == 0 else i + 1, 1 - b, range(0, 2))
                    if is_last(m):
                        pe.wait_ge(s["msg_ready"], C * m + c + 1)
                    else:
                        pe.wait_ge(s["h_silu"], C * (m + 1) + c + 1)
                    w = slice(P * c, P * c + P)
                    layer_chunk(pe, bank[c][:, e],
                                lambda k: ((wn1_lo[:, k, w], agg_hi[:, k, e]), (wn1_hi[:, k, w], agg_hi[:, k, e]),
                                           (wn1_hi[:, k, w], agg_lo[:, k, e])),
                                ("agg_hi_ready", "agg_lo_ready", C * m) if c == 0 else None
                                ).then_inc(s["u_mm"], 1)
                if not is_last(m):
                    row_transposes(m + 1, i if b == 0 else i + 1, 1 - b, range(2, C))
                    mask(m + 1)
                for j in range(J):
                    pe.wait_ge(s["u_silu"], C * m + j + 1)
                    n = edge_rows(m, j)
                    w = slice(P * j, P * j + n)
                    layer_chunk(pe, bank[j][0:n, :],
                                lambda k: ((u_hi[:, k, w], wn2_lo[:, k, :]), (u_hi[:, k, w], wn2_hi[:, k, :]),
                                           (u_lo[:, k, w], wn2_hi[:, k, :])),
                                ("u_silu", "u_lo_ready", C * m) if j == 0 else None).then_inc(s["y_mm"], 1)

            steps(pe, step)

        @block.vector
        def _(dve):
            dve.wait_ge(s["numbers_ready"], 2)
            dve.wait_ge(s["src_in"], 16)
            nc.vector.tensor_scalar(node_part[:, 0, :], edge_int[:, 2, :], 7, None, ALU.logical_shift_right
                                    ).then_inc(s["parts"], 1)
            nc.vector.tensor_scalar(node_part[:, 1, :], edge_int[:, 2, :], P - 1, None, ALU.bitwise_and
                                    ).then_inc(s["parts"], 1)
            dve.wait_ge(s["parts"], 2)

            def one_hot(target, width, number, n):
                shape = [RP, n, width]
                return nc.vector.tensor_tensor(target, iota_int[0:RP, 0:width].unsqueeze(1).broadcast_to(shape),
                                               number.unsqueeze(2).broadcast_to(shape), ALU.is_equal)

            for q in range(ROUNDS):
                t = slice(8 * q, 8 * q + 8)
                one_hot(is_hi[:, t, :], HI, node_part[:, 0, t], 8).then_inc(s["one_hots"], 1)
                one_hot(is_lo[:, t, :], P, node_part[:, 1, t], 8).then_inc(s["one_hots"], 1)
            for g in range(POOL_COPIES, GROUPS):
                t = slice(4 * g, 4 * g + 4)
                dve.wait_ge(s["hi_T_ready"], g + 1)
                nc.vector.tensor_copy(is_hi_T_bf[:, t, :], is_hi_T[:, t, 0:RP].bitcast(F32)
                                      ).then_inc(s["hi_T_bf_dve"], 1)
            dve.wait_ge(s["pool_const"], POOL_CONSTS)
            dve.wait_ge(s["counted_mm"], 3)
            nc.vector.tensor_tensor_scan(up_to[:, :], ones[:, :], counted(GROUPS), zero_col[:, 0:1], ALU.mult, ALU.add
                                         ).then_inc(s["up_to_ready"], 1)
            nc.vector.tensor_copy(total[:, :], counted(GROUPS)).then_inc(s["total_copied"], 1)
            dve.wait_ge(s["below_mm"], 1)
            nc.vector.tensor_scalar(below[:, :], bank[4][0:HI, 0:1], -float(CENTRE), None, ALU.add
                                    ).then_inc(s["start_chain"], 1)
            dve.wait_ge(s["start_chain"], 1)
            dve.wait_ge(s["total_copied"], 1)
            nc.vector.scalar_tensor_tensor(out=start[:, :], in0=up_to[:, :], scalar=below[:, 0:1], in1=total[:, :],
                                           op0=ALU.add, op1=ALU.subtract).then_inc(s["start_chain"], 1)
            dve.wait_ge(s["start_chain"], 2)
            nc.vector.tensor_copy(group_start[:, 0, :], start[:, :]).then_inc(s["start_ready"], 1)
            for n, b in enumerate((0, 1, 3)):
                first, last = 4 * n + 1, min(4 * n + 4, GROUPS - 1)
                k = last - first + 1
                nc.vector.tensor_tensor(group_start[:, first:last + 1, :],
                                        bank[b][0:HI, 0:P * k].rearrange("p (k n) -> p k n", k=k),
                                        start[:, :].unsqueeze(1).broadcast_to([HI, k, P]), ALU.add
                                        ).then_inc(s["start_ready"], 1)
            dve.wait_ge(s["dst_in"], 16)
            nc.vector.tensor_scalar(low_int[:, :, :], edge_int[:, :, :], LOW - 1, None, ALU.bitwise_and
                                    ).then_inc(s["vals_ready"], 1)
            nc.vector.tensor_scalar(high_int[:, :, :], edge_int[:, :, :], 12, None, ALU.logical_shift_right
                                    ).then_inc(s["vals_ready"], 1)
            dve.wait_ge(s["vals_ready"], 2)
            nc.vector.tensor_scalar(vals[:, :, 0:3].rearrange("p t v -> p v t"), low_int[:, :, :],
                                    -float(LOW // 2), None, ALU.add).then_inc(s["vals_ready"], 1)
            nc.vector.scalar_tensor_tensor(out=high_two[:, :], in0=high_int[:, 1, :], scalar=4.0,
                                           in1=high_int[:, 0, :], op0=ALU.mult, op1=ALU.add
                                           ).then_inc(s["vals_ready"], 1)
            dve.wait_ge(s["vals_ready"], 4)
            nc.vector.scalar_tensor_tensor(out=vals[:, :, 3], in0=high_int[:, 2, :], scalar=16.0,
                                           in1=high_two[:, :], op0=ALU.mult, op1=ALU.add
                                           ).then_inc(s["vals_ready"], 1)
            def place(q, stage):
                r = slice(8 * q, 8 * q + 8)
                if stage == 0:
                    dve.wait_ge(s["found_done"], 8 * q + 8)
                    nc.vector.tensor_scalar(pos_int[:, 0, r], found[:, r], float(CENTRE), None, ALU.add
                                            ).then_inc(s["rank_chain"], 1)
                elif stage == 1:
                    dve.wait_ge(s["rank_chain"], 3 * q + 1)
                    nc.vector.tensor_scalar(pos_int[:, 1, r], pos_int[:, 0, r], 7, None, ALU.logical_shift_right
                                            ).then_inc(s["rank_chain"], 1)
                    nc.vector.tensor_scalar(pos_int[:, 2, r], pos_int[:, 0, r], P - 1, None, ALU.bitwise_and
                                            ).then_inc(s["rank_chain"], 1)
                elif stage == 2:
                    dve.wait_ge(s["rank_chain"], 3 * q + 3)
                    need(dve, "spread_ready", q - 2)
                    one_hot(is_tile[:, q % 3, :, :], TILES, pos_int[:, 1, r], 8).then_inc(s["is_tile_ready"], 1)
                else:
                    need(dve, "index_mm", q - 2)
                    one_hot(is_slot[:, q % 3, :, :], P, pos_int[:, 2, r], 8).then_inc(s["is_slot_ready"], 1)

            for q in range(ROUNDS):
                for k in range(8):
                    t = 8 * q + k
                    dve.wait_ge(s["find_mm"], t // 4 + 1)
                    need(dve, "found_done", t - 3)
                    nc.vector.scalar_tensor_tensor(
                        out=scrap[:, t % 4, :], in0=bank[(4, 6)[t // 4 % 2]][0:RP, P * (t % 4):P * (t % 4) + P],
                        scalar=1.0, in1=is_lo[:, t, :], op0=ALU.mult, op1=ALU.mult,
                        accum_out=found[:, t:t + 1]).then_inc(s["found_done"], 1)
                    if q and k % 2 == 0:
                        place(q - 1, k // 2)
                if q == 0:
                    dve.wait_ge(s["total_T_ready"], 1)
                    nc.vector.tensor_scalar(touched[:, :], total_T[:, :], 1.0, float(FAR), ALU.min, ALU.mult
                                            ).then_inc(s["base_index_ready"], 1)
                    dve.wait_ge(s["base_index_ready"], 1)
                    nc.vector.tensor_tensor(base_index[:, 0:HI], node_int[:, 0:HI], touched[:, :], ALU.add
                                            ).then_inc(s["base_index_ready"], 1)
                    dve.wait_ge(s["mid_split"], 1)
                    nc.vector.tensor_tensor(mid_lo[:, :], mid[:, :], mid_hi[:, :].bitcast(F32),
                                            ALU.subtract).then_inc(s["mid_low"], 1)
            for stage in range(4):
                place(ROUNDS - 1, stage)
            dve.wait_ge(s["is_tile_ready"], ROUNDS)
            spread_tiles(nc.vector, ROUNDS - 1, 4, 8).then_inc(s["spread_end"], 1)
            dve.wait_ge(s["index_mm"], ROUNDS)
            nc.vector.tensor_scalar(sorted_low[:, :, :].rearrange("p v a -> p (v a)"), bank[5][:, 0:3 * TILES],
                                    float(LOW // 2), None, ALU.add).then_inc(s["index_chain"], 1)
            nc.vector.tensor_copy(sorted_high[:, :], bank[5][:, 3 * TILES:4 * TILES]).then_inc(s["index_chain"], 1)
            dve.wait_ge(s["index_chain"], 2)
            for v in range(3):
                nc.vector.tensor_scalar(sorted_top[:, v, :], sorted_high[:, :], 3 << (2 * v), 12 - 2 * v,
                                        ALU.bitwise_and, ALU.logical_shift_left).then_inc(s["index_chain"], 1)
            dve.wait_ge(s["index_chain"], 5)
            nc.vector.tensor_tensor(src_sorted[:, 1:TILES + 1], sorted_low[:, 2, :], sorted_top[:, 2, :], ALU.add
                                    ).then_inc(s["index_chain"], 1)
            nc.vector.tensor_tensor(gather_index[:, 0:2, :], sorted_low[:, 0:2, :], sorted_top[:, 0:2, :], ALU.add
                                    ).then_inc(s["edges_ready"], 1)
            dve.wait_ge(s["index_chain"], 6)
            nc.vector.tensor_tensor(src_sorted[:, TILES:TILES + 1], src_sorted[:, TILES:TILES + 1],
                                    pad_far[:, :], ALU.add).then_inc(s["src_sorted_ready"], 1)
            dve.wait_ge(s["src_sorted_ready"], 1)
            nc.vector.tensor_scalar(gather_index[:, 2, :], src_sorted[:, 1:TILES + 1], float(N - 1), None,
                                    ALU.min).then_inc(s["index_chain"], 1)
            dve.wait_ge(s["shift_mm"], 2)
            nc.vector.tensor_tensor(same_as_next[:, :], bank[7][:, 0:TILES], src_sorted[:, 1:TILES + 1],
                                    ALU.is_equal).then_inc(s["index_chain"], 1)
            nc.vector.tensor_tensor(same_as_before[:, :], bank[2][:, 0:TILES], src_sorted[:, 1:TILES + 1],
                                    ALU.is_equal).then_inc(s["index_chain"], 1)
            dve.wait_ge(s["index_chain"], 9)
            nc.vector.scalar_tensor_tensor(out=store_index[:, :], in0=same_as_next[:, :], scalar=float(FAR),
                                           in1=src_sorted[:, 1:TILES + 1], op0=ALU.mult, op1=ALU.add
                                           ).then_inc(s["index_ready"], 1)
            def weight_low(name, hi, lo, raw, n, done):
                dve.wait_ge(s[name], n)
                nc.vector.tensor_tensor(lo, raw, hi.bitcast(F32), ALU.subtract).then_inc(s[done], 1)

            weight_low("we_hi", we1_hi[:, :], we1_lo[:, :], we1_raw[:, :], 1, "we_lo")
            for c in range(C):
                weight_low("we_hi", we2_hi[:, c, :], we2_lo[:, c, :], we2_raw[:, c, :], c + 2, "we_lo")
            dve.wait_ge(s["row_mm"], 1)
            dve.wait_ge(s["bn2_halved"], 1)
            nc.vector.scalar_tensor_tensor(out=row_half[:, :], in0=bank[3][:, :], scalar=0.5,
                                           in1=bn2_half[:, :], op0=ALU.mult, op1=ALU.add
                                           ).then_inc(s["row_ready"], 1)
            def low(target, whole, high, name):
                nc.vector.tensor_tensor(target, whole, high.bitcast(F32), ALU.subtract).then_inc(s[name], 1)

            def split_attr(m):
                dve.wait_ge(s["attr_T_hi_ready"], m + 1)
                w = slice(0, width(m))
                low(attr_T_lo[:, w], bank[4][:, w], attr_T_hi[:, w], "attr_T_lo_ready")

            def hidden_low(m, bias=False):
                for c in range(C):
                    dve.wait_ge(s["h_silu"], C * m + c + 1)
                    w = slice(0, width(m))
                    low(h_lo[:, c, w], silu[:, c % 2, w], h_hi[:, c, w], "h_lo_ready")
                    if bias:
                        bias_rows(m - 1, c)

            def agg_low(m, c):
                dve.wait_ge(s["agg_hi_ready"], C * m + c + 1)
                w = slice(0, width(m))
                low(agg_lo[:, c, w], agg_T[:, c % 2, w], agg_hi[:, c, w], "agg_lo_ready")

            def base_add(m, i, b, half, k, name):
                n = base_rows(m, half, k)
                if k == 0:
                    dve.wait_ge(base_in[b][half], 16 * (i + 1) + (16 if base_rows(m, half, J - 1) < P and n == P
                                                                  and isinstance(m, int) else 0))
                if n:
                    t = base[0:n, b, half, k, :]
                    nc.vector.tensor_tensor(t, t, row_half[0:n, :], ALU.add).then_inc(s[name], 1)

            def moments(m, which, k, n, rows, stat, aggr, eps, tiles):
                nc.vector.bn_stats(stats[0:n, which, k, :], rows).then_inc(s[stat], 1)
                need(dve, stat, J * m + k + 1, True)
                nc.vector.bn_aggr(mean_var[0:n, which, k, :], stats[0:n, which, k, :]).then_inc(s[aggr], 1)
                if tiles:
                    need(dve, "rstd_ready", 2 * (m - 1) + (1 if which == HALF_A else 2))
                    dve.wait_ge(s[aggr], J * m + k + 1)
                    nc.vector.tensor_scalar(var_eps[:, which, tiles], mean_var[:, which, tiles, 1], eps, None,
                                            ALU.add).then_inc(s["var_ready"], 1)

            def base_moments(m, b, half, k, added, which, stat, aggr):
                n = base_rows(m, half, k)
                if n:
                    dve.wait_ge(s[added], J * m + k + 1)
                    end = k == J - 1 or not base_rows(m, half, k + 1)
                    moments(m, which, k, n, base[0:n, b, half, k, :], stat, aggr, EPS / 4,
                            slice(0, J) if end else None)

            def shift_of(which, m):
                dve.wait_ge(s["rstd_ready"], moments_made(which, m))
                nc.vector.scalar_tensor_tensor(out=group(shift, which, m), in0=group(mean_var[:, :, :, 0], which, m),
                                               scalar=-1.0, in1=group(rstd, which, m), op0=ALU.mult, op1=ALU.mult
                                               ).then_inc(s["shift_ready"], 1)

            def bias_rows(m, j):
                dve.wait_ge(s["xs_in"], 16 * J * (m + 1))
                nc.vector.tensor_tensor(xs[:, j, :], xs[:, j, :], bn2_half[:, :], ALU.add
                                        ).then_inc(s["xs_biased"], 1)

            dve.wait_ge(s["be2_in"], 16)
            split_attr(0)
            for c in range(C):
                weight_low("wn1_hi", wn1_hi[:, c, :], wn1_lo[:, c, :], wn1_raw[:, c, :], c + 1, "wn1_lo")
            hidden_low(0)

            def step(m, i, b):
                w = slice(0, width(m))
                if not is_last(m):
                    split_attr(m + 1)
                for c in range(C):
                    dve.wait_ge(s["ef_mm"], C * m + c + 1)
                    dve.wait_ge(s["xd_T_ready"], C * m + c + 1)
                    nc.vector.scalar_tensor_tensor(out=msg_T[:, c % 2, w], in0=bank[c][:, w],
                                                   scalar=be2_col[:, c:c + 1], in1=xd_T[:, c, w],
                                                   op0=ALU.add, op1=ALU.mult).then_inc(s["msg_ready"], 1)
                    if c == 0:
                        dve.wait_ge(s["mask_mm"], m + 1)
                        need(dve, "u_mm", C * m)
                        need(dve, "carried", C * m)
                    else:
                        agg_low(m, c - 1)
                    dve.wait_ge(s["msg_ready"], C * m + c + 1)
                    nc.vector.tensor_tensor_scan(agg_T[:, c % 2, w], bank[7][:, w], msg_T[:, c % 2, w],
                                                 carry[:, c:c + 1], ALU.mult, ALU.add
                                                 ).then_inc(s["scan_done"], 1)
                    if c == 0 and not (isinstance(m, int) and m == 0):
                        shift_of(HALF_B, m - 1)
                    if is_last(m):
                        base_add(m, i, b, 1, c, "base_added_b")
                    else:
                        dve.wait_ge(s["scan_done"], C * m + c + 1)
                        nc.vector.tensor_copy(carry[:, c:c + 1], agg_T[:, c % 2, M - 1:M]).then_inc(s["carried"], 1)
                agg_low(m, C - 1)
                if is_last(m):
                    for j in range(J):
                        base_moments(m, b, 1, j, "base_added_b", HALF_B, "stats_b", "aggr_b")
                    for j in range(J):
                        bias_rows(m, j)
                else:
                    hidden_low(m + 1, True)
                base_moments(m, b, 0, 0, "base_added_a", HALF_A, "stats_a", "aggr_a")
                for c in range(C):
                    dve.wait_ge(s["u_silu"], C * m + c + 1)
                    low(u_lo[:, c, w], silu[:, c % 2, w], u_hi[:, c, w], "u_lo_ready")
                    if not is_last(m):
                        base_add(m, i, b, 1, c, "base_added_b")
                    if c < C - 1:
                        base_moments(m, b, 0, c + 1, "base_added_a", HALF_A, "stats_a", "aggr_a")
                    elif is_last(m):
                        shift_of(HALF_B, m)
                for j in range(J):
                    if not is_last(m):
                        base_moments(m, b, 1, j, "base_added_b", HALF_B, "stats_b", "aggr_b")
                    elif j == J - 1:
                        shift_of(OUT, m)
                    dve.wait_ge(s["y_mm"], C * m + j + 1)
                    if j == 0:
                        dve.wait_ge(s["xs_biased"], J * (m + 1))
                        need(dve, "out_stored", 16 * J * m)
                    n = edge_rows(m, j)
                    nc.vector.scalar_tensor_tensor(out=z[0:n, j, :], in0=xs[0:n, j, :], scalar=2.0,
                                                   in1=bank[j][0:n, :], op0=ALU.mult, op1=ALU.add
                                                   ).then_inc(s["z_ready"], 1)
                    dve.wait_ge(s["z_ready"], J * m + j + 1)
                    ends = ({SPLIT - 1: slice(0, SPLIT), J - 1: slice(SPLIT, J)} if is_last(m)
                            else {J - 1: slice(0, J)})
                    moments(m, OUT, j, n, z[0:n, j, :], "stats_out", "aggr_out", EPS, ends.get(j))
                    if j == 0:
                        shift_of(HALF_A, m)

            steps(dve, step)
            shift_of(OUT_END, MACROS - 1)


POOL_CONSTS = 22


_INS = ["x", "src", "dst", "edge_attr_128", "L0_gnn_We1", "L0_gnn_be1", "L0_gnn_We2", "L0_gnn_be2",
        "L0_gnn_Wn1", "L0_gnn_bn1", "L0_gnn_Wn2", "L0_gnn_bn2"]


def kernel(**inputs):
    import numpy as np
    import concourse.bacc as bacc
    from concourse.bass_utils import run_bass_kernel_spmd

    nc = bacc.Bacc("TRN2", target_bir_lowering=False, num_devices=1)
    arrays, args = {}, []
    for name in _INS:
        a = np.ascontiguousarray(inputs[name])
        arrays[f"in_{name}"] = a
        args.append(nc.dram_tensor(f"in_{name}", a.shape, mybir.dt.from_np(a.dtype), kind="ExternalInput").ap())
    shape = arrays["in_x"].shape
    args.append(nc.dram_tensor("out_rows", shape, F32, kind="ExternalOutput").ap())
    gnn_kernel(nc, *args)
    r = run_bass_kernel_spmd(nc, [arrays], core_ids=[0])
    return r.results[0]["out_rows"]
```
